# Optimizing a Trainium2 kernel written in Bass

```python
import numpy as np
import jax
import jax.numpy as jnp

def _softmax(x, axis=-1):
    return jax.nn.softmax(x, axis=axis)

def _gelu(x):
    return jax.nn.gelu(x, approximate=True)

def _silu(x):
    return jax.nn.silu(x)

def _sigmoid(x):
    return jax.nn.sigmoid(x)

def _layernorm(x, axis=-1, eps=1e-05):
    m = jnp.mean(x, axis=axis, keepdims=True)
    v = jnp.var(x, axis=axis, keepdims=True)
    return (x - m) / jnp.sqrt(v + eps)

def _scatter_add(tgt, idx, src, axis=0):
    return tgt.at[idx].add(src)

def _segment_sum(src, seg, n):
    return jax.ops.segment_sum(src, seg, n)
kernel_name = 'mk_xattn_ffn_d1_seqx_r4_7cc1a6'

def setup_inputs(seed: int=0):
    np.random.seed(seed)
    _w = jnp.asarray

    def _rec_inputs():
        import jax
        import jax.numpy as jnp
        _rk = jax.random.key(seed)
        x = 7.22e-05 + 1 * jax.random.normal(jax.random.fold_in(_rk, 1), (4, 1024, 256), jnp.float32)
        _lenS = 1024 - jax.random.randint(jax.random.fold_in(_rk, 7), (4,), 0, max(1, 1024 // 4) + 1, jnp.int32)
        _lenS2 = 77 - jax.random.randint(jax.random.fold_in(_rk, 8), (4,), 0, max(1, 77 // 4) + 1, jnp.int32)
        _ctx_1024P = jax.random.normal(jax.random.fold_in(_rk, 11), (4, 16, 256), jnp.float32)
        _ctx_1024c = jax.random.dirichlet(jax.random.fold_in(_rk, 511), 0.3 * jnp.ones((16,), jnp.float32), (4, 77))
        _ctx_1024t = jnp.einsum('bsk,bkd->bsd', _ctx_1024c, _ctx_1024P)
        _ctx_1024t = _ctx_1024t * jax.lax.rsqrt(jnp.mean(jnp.square(_ctx_1024t)) + 1e-12) * 0.953939
        ctx_1024 = 4.13588e-05 + 0.999923 * (_ctx_1024t + 0.3 * jax.random.normal(jax.random.fold_in(_rk, 611), (4, 77, 256), jnp.float32))
        return (x, ctx_1024)
    x, ctx_1024 = _rec_inputs()

    def _L0_xattn_setup():
        import jax, jax.numpy as jnp
        import numpy as np
        INPUTQ_DIM = 256
        EMBED_DIM = 256
        NUM_HEADS = 16
        HEAD_DIM = EMBED_DIM // NUM_HEADS

        def _xavier(key, shape):
            fan_out, fan_in = shape
            limit = float(np.sqrt(6.0 / (fan_in + fan_out)))
            return jax.random.uniform(key, shape, jnp.float32, -limit, limit)
        key = jax.random.key(seed)
        ks = jax.random.split(key, 5)
        B, Nq, N = (4, 512, 512)
        return {'input_q': jax.random.normal(ks[0], (B, Nq, INPUTQ_DIM), jnp.float32), 'input_kv': jax.random.normal(ks[1], (B, N, EMBED_DIM), jnp.float32), 'w_q': _xavier(ks[2], (EMBED_DIM, INPUTQ_DIM)), 'b_q': jnp.zeros((EMBED_DIM,), jnp.float32), 'w_kv': _xavier(ks[3], (2 * EMBED_DIM, EMBED_DIM)), 'b_kv': jnp.zeros((2 * EMBED_DIM,), jnp.float32), 'w_out': _xavier(ks[4], (INPUTQ_DIM, EMBED_DIM)), 'b_out': jnp.zeros((INPUTQ_DIM,), jnp.float32)}
    _L0_xattn_all = _L0_xattn_setup()
    _L0_xattn_in = {k: v for k, v in _L0_xattn_all.items() if k in ('w_q', 'b_q', 'w_kv', 'b_kv', 'w_out', 'b_out')}
    del _L0_xattn_all

    def _L0_ffn_setup():
        import jax, jax.numpy as jnp
        import numpy as np
        TOP_K = 2
        CAP_FACTOR = 1.25
        EPS = 1.1920929e-07
        key = jax.random.key(seed)
        ks = jax.random.split(key, 6)
        B, S, D, E, H = (8, 512, 256, 8, 1024)
        return {'hidden_states': jax.random.normal(ks[0], (B, S, D), jnp.float32), 'wg': jax.random.normal(ks[1], (D, E), jnp.float32) * 0.02, 'fc1_w': jax.random.normal(ks[2], (E, H, D), jnp.float32) * 0.02, 'fc1_b': jnp.zeros((E, H), jnp.float32), 'fc2_w': jax.random.normal(ks[3], (E, H, D), jnp.float32) * 0.02, 'fc2_b': jnp.zeros((E, D), jnp.float32), 'ln_gamma': jnp.ones((D,), jnp.float32), 'ln_beta': jnp.zeros((D,), jnp.float32)}
    _L0_ffn_all = _L0_ffn_setup()
    _L0_ffn_in = {k: v for k, v in _L0_ffn_all.items() if k in ('wg', 'fc1_w', 'fc1_b', 'fc2_w', 'fc2_b', 'ln_gamma', 'ln_beta')}
    del _L0_ffn_all
    return {'x': x, 'ctx_1024': ctx_1024, 'L0_xattn_w_q': _L0_xattn_in['w_q'], 'L0_xattn_b_q': _L0_xattn_in['b_q'], 'L0_xattn_w_kv': _L0_xattn_in['w_kv'], 'L0_xattn_b_kv': _L0_xattn_in['b_kv'], 'L0_xattn_w_out': _L0_xattn_in['w_out'], 'L0_xattn_b_out': _L0_xattn_in['b_out'], 'L0_ffn_wg': _L0_ffn_in['wg'], 'L0_ffn_fc1_w': _L0_ffn_in['fc1_w'], 'L0_ffn_fc1_b': _L0_ffn_in['fc1_b'], 'L0_ffn_fc2_w': _L0_ffn_in['fc2_w'], 'L0_ffn_fc2_b': _L0_ffn_in['fc2_b'], 'L0_ffn_ln_gamma': _L0_ffn_in['ln_gamma'], 'L0_ffn_ln_beta': _L0_ffn_in['ln_beta']}

def reference(x, ctx_1024, L0_xattn_w_q, L0_xattn_b_q, L0_xattn_w_kv, L0_xattn_b_kv, L0_xattn_w_out, L0_xattn_b_out, L0_ffn_wg, L0_ffn_fc1_w, L0_ffn_fc1_b, L0_ffn_fc2_w, L0_ffn_fc2_b, L0_ffn_ln_gamma, L0_ffn_ln_beta):
    import jax
    import jax.numpy as jnp

    def _L0_xattn_ref(input_q, input_kv, w_q, b_q, w_kv, b_kv, w_out, b_out):
        import jax, jax.numpy as jnp
        import numpy as np
        INPUTQ_DIM = 256
        EMBED_DIM = 256
        NUM_HEADS = 16
        HEAD_DIM = EMBED_DIM // NUM_HEADS

        def _xavier(key, shape):
            fan_out, fan_in = shape
            limit = float(np.sqrt(6.0 / (fan_in + fan_out)))
            return jax.random.uniform(key, shape, jnp.float32, -limit, limit)
        B, N, _ = input_kv.shape
        _, Nq, _ = input_q.shape
        H, Dh = (NUM_HEADS, HEAD_DIM)
        q = (input_q @ w_q.T + b_q).reshape(B, Nq, H, Dh).transpose(0, 2, 1, 3)
        kv = (input_kv @ w_kv.T + b_kv).reshape(B, N, H, 2 * Dh).transpose(0, 2, 1, 3)
        k, v = (kv[..., :Dh], kv[..., Dh:])
        scores = jnp.einsum('bhqd,bhkd->bhqk', q, k) / jnp.sqrt(jnp.float32(Dh))
        attn = jax.nn.softmax(scores, axis=-1)
        values = jnp.einsum('bhqk,bhkd->bhqd', attn, v)
        values = values.transpose(0, 2, 1, 3).reshape(B, Nq, EMBED_DIM)
        out = values @ w_out.T + b_out
        return out

    def _L0_ffn_ref(hidden_states, wg, fc1_w, fc1_b, fc2_w, fc2_b, ln_gamma, ln_beta):
        import jax, jax.numpy as jnp
        import numpy as np
        TOP_K = 2
        CAP_FACTOR = 1.25
        EPS = 1.1920929e-07
        B, S, D = hidden_states.shape
        E = wg.shape[1]
        N = B * S
        k = TOP_K
        C = k * int(CAP_FACTOR * ((N + E - 1) // E))
        x = hidden_states.reshape(N, D)
        scores = jax.nn.softmax(x @ wg, axis=-1)
        gates, idx = jax.lax.top_k(scores, k)
        gates = gates / jnp.clip(jnp.sum(gates, -1, keepdims=True), EPS)
        masks = jax.nn.one_hot(idx, E, dtype=jnp.int32)
        counts = masks.sum(0)
        offsets = jnp.concatenate([jnp.zeros((1, E), jnp.int32), jnp.cumsum(counts, 0)[:-1]], 0)
        loc = jnp.cumsum(masks, 0) - 1 + offsets[None]
        loc_sel = (loc * masks).sum(-1)
        keep = loc_sel < C
        gates = gates * keep.astype(gates.dtype)
        pos = jnp.where(keep, idx * C + loc_sel, E * C)
        xk = jnp.broadcast_to(x[:, None, :], (N, k, D)).reshape(N * k, D)
        buf = jnp.zeros((E * C + 1, D), x.dtype).at[pos.reshape(-1)].set(xk)
        disp = buf[:E * C].reshape(E, C, D)
        h = jax.nn.silu(jnp.einsum('ecd,ehd->ech', disp, fc1_w) + fc1_b[:, None, :])
        y = jnp.einsum('ech,ehd->ecd', h, fc2_w) + fc2_b[:, None, :]
        ybuf = jnp.concatenate([y.reshape(E * C, D), jnp.zeros((1, D), y.dtype)], 0)
        combined = jnp.sum(gates[..., None] * ybuf[pos], axis=1)
        res = hidden_states + combined.reshape(B, S, D)
        mu = jnp.mean(res, -1, keepdims=True)
        var = jnp.var(res, -1, keepdims=True)
        return (res - mu) * jax.lax.rsqrt(var + 1e-05) * ln_gamma + ln_beta
    x = x + _L0_xattn_ref(_layernorm(x, axis=-1), ctx_1024, L0_xattn_w_q, L0_xattn_b_q, L0_xattn_w_kv, L0_xattn_b_kv, L0_xattn_w_out, L0_xattn_b_out)
    x = x + _L0_ffn_ref(_layernorm(x, axis=-1), L0_ffn_wg, L0_ffn_fc1_w, L0_ffn_fc1_b, L0_ffn_fc2_w, L0_ffn_fc2_b, L0_ffn_ln_gamma, L0_ffn_ln_beta)
    return x

_drawn_inputs = setup_inputs


def setup_inputs(seed=0):
    import zlib

    import numpy as np

    out = dict(_drawn_inputs(seed))
    spreads = {'L0_xattn_b_q': (0.0, 0.541),
     'L0_xattn_b_kv': (0.0, 0.1),
     'L0_xattn_b_out': (0.0, 0.1),
     'L0_ffn_fc1_b': (0.0, 0.696),
     'L0_ffn_fc2_b': (0.0, 0.1),
     'L0_ffn_ln_gamma': (1.0, 0.2),
     'L0_ffn_ln_beta': (0.0, 0.1)}
    factors = {}
    for name, (base, spread) in spreads.items():
        noise = np.random.default_rng([zlib.crc32(name.encode()), seed]).standard_normal(out[name].shape)
        drawn = base * np.exp(spread * noise) if base else spread * noise
        out[name] = jnp.asarray(drawn.astype(out[name].dtype))
    for name, factor in factors.items():
        out[name] = (out[name] * factor).astype(out[name].dtype)
    return out
```

```python
import concourse.bass as bass
from concourse import mybir
from contextlib import ExitStack


def xattn_moe_kernel(nc, x, ctxT, wqT, bq, wkT, bk, wvT, bv, woT, bo, wg, w1T, b1T, w2, b2, gamma, beta, out):
    f32, f32r, bf16, i32 = mybir.dt.float32, mybir.dt.float32r, mybir.dt.bfloat16, mybir.dt.int32
    ALU, ACT, AX = mybir.AluOpType, mybir.ActivationFunctionType, mybir.AxisListType.X
    ds = bass.ds

    P = 128
    N, D = x.shape
    NT = N // P
    DC = D // P
    _, NB, NK = ctxT.shape
    TPB = NT // NB
    NH, DH = 16, 16
    HH = NH // 2
    KC = HH // 2 * NK
    KH = HH * NK
    NJ = 5
    JW = 124
    JS = JW - 1
    VW = P + HH
    assert JS * (NJ - 1) + JW == KH
    NE, _, HID = w1T.shape
    HJ = HID // P
    CAP = 2 * int(1.25 * ((N + NE - 1) // NE))
    NS = NE * CAP // P
    NST = NS // 2
    SPE = CAP // (2 * P)
    NR = 2
    NC = NR * NT
    EPS_LN, EPS_GATE = 1e-5, 1.1920929e-07
    SCALE = float(DH) ** -0.5
    PAIRS = NT // 2

    xn_rows = nc.dram_tensor("xn_rows", [N, D], f32, kind="Internal").ap()
    sum_rows = nc.dram_tensor("sum_rows", [N + 4 * P, D], f32, kind="Internal").ap()
    gate_rows = nc.dram_tensor("gate_rows", [P * NC, 1], f32, kind="Internal").ap()
    x_t = x.rearrange("(t p) d -> p t d", p=P)
    xn_t = xn_rows.rearrange("(t p) d -> p t d", p=P)
    out_t = out.rearrange("(t p) d -> p t d", p=P)
    sum_t = sum_rows[0:N, :].rearrange("(t p) d -> p t d", p=P)

    def wait(engine, sem, value):
        if not isinstance(value, int) or value > 0:
            engine.wait_ge(sem, value)

    def in_register(engine, value):
        return value if isinstance(value, int) else engine.snap(value)

    def within(t, n):
        return not isinstance(t, int) or 0 <= t < n

    def row(ap):
        return ap.rearrange("(a n) -> a n", a=1).to_broadcast([P, ap.shape[0]])

    sems = {}

    root, only_attn, only_moe = ExitStack(), ExitStack(), ExitStack()
    with root:
        def sb(name, shape, dt=f32, where=root):
            return where.enter_context(nc.sbuf_tensor(name, shape, dt))

        X = sb("X", [P, NT, D])
        w1raw = sb("w1raw", [P, DC, HID])
        w2raw = sb("w2raw", [P, HJ, D])
        ident = sb("ident", [P, P])
        logits = sb("logits", [P, NT, NE])
        gates = sb("gates", [P, NR, NT])
        slot_ids = sb("slot_ids", [P, NST, 3, 2], i32)
        b1_sb = sb("b1_sb", [P, NE * HJ])
        b1_now = sb("b1_now", [P, 2, HJ])
        minus_half = sb("minus_half", [P, 4])
        upper = sb("upper", [P, P], bf16)
        gamma_sb, beta_sb = sb("gamma_sb", [P, D]), sb("beta_sb", [P, D])
        ones_bf = sb("ones_bf", [P, P], bf16)
        iota_lo = sb("iota_lo", [P, P], bf16)
        iota_hi = sb("iota_hi", [P, NS], bf16)
        my_row = sb("my_row", [P, 1])

        A = only_attn
        KH_hi = sb("KH_hi", [P, NB * 2 * KH], f32r, A)
        KH_lo = sb("KH_lo", [P, NB * 2 * KH], f32r, A)
        VB = sb("VB", [JW, NB * 2 * NJ * VW], f32, A)
        probs = sb("probs", [P, 2, 2 * KH], f32, A)
        probsT = sb("probsT", [JW, 2 * NJ, P], f32, A)
        ctx_sb = sb("ctx_sb", [P, DC, NB * NK], f32, A)
        wq_sb, wk_sb, wv_sb, wo_sb = (sb(n, [P, DC, D], f32, A) for n in ("wq_sb", "wk_sb", "wv_sb", "wo_sb"))
        wq_hi, wq_lo, wo_hi, wo_lo = (sb(n, [P, DC, D], f32r, A) for n in ("wq_hi", "wq_lo", "wo_hi", "wo_lo"))
        wg_sb = sb("wg_sb", [P, DC, P], f32, A)
        bq_sb, bk_sb = sb("bq_sb", [P, DC], f32, A), sb("bk_sb", [P, DC], f32, A)
        bv_sb, bo_sb = sb("bv_sb", [P, D], f32, A), sb("bo_sb", [P, D], f32, A)
        kT = sb("kT", [P, DC, NB * NK], f32, A)
        kT_hi, kT_lo = sb("kT_hi", [P, DC, NB * NK], f32r, A), sb("kT_lo", [P, DC, NB * NK], f32, A)
        v_sb = sb("v_sb", [NK, NB, D], f32, A)
        key_of_row = sb("key_of_row", [NK, HH, NK], f32, A)
        head_of_feature = sb("head_of_feature", [P, HH], f32, A)
        head_of_row = sb("head_of_row", [JW, NJ, HH], f32, A)
        xn1 = sb("xn1", [P, 2, D], f32, A)
        xn1T_hi, xn1T_lo = sb("xn1T_hi", [P, DC, 2 * P], f32r, A), sb("xn1T_lo", [P, DC, 2 * P], f32r, A)
        q_hi, q_lo = sb("q_hi", [P, DC, 2 * P], f32r, A), sb("q_lo", [P, DC, 2 * P], f32r, A)
        rowmax = sb("rowmax", [P, 2, HH], f32, A)
        rden = sb("rden", [P, 2, HH], f32, A)
        vals = sb("vals", [P, D], f32, A)
        valsT_hi, valsT_lo = sb("valsT_hi", [P, DC, P], f32r, A), sb("valsT_lo", [P, DC, P], f32r, A)
        xn2 = sb("xn2", [P, 2, D], f32, A)
        xn2T = sb("xn2T", [P, DC, P], f32, A)
        zero_row = sb("zero_row", [P, D], f32, A)
        st1, mv1 = sb("st1", [P, 2, 6], f32, A), sb("mv1", [P, 2, 2], f32, A)
        var1, rstd1 = sb("var1", [P, 2], f32, A), sb("rstd1", [P, 2], f32, A)
        st2, mv2 = sb("st2", [P, 2, 6], f32, A), sb("mv2", [P, 2, 2], f32, A)
        var2, rstd2 = sb("var2", [P, 2], f32, A), sb("rstd2", [P, 2], f32, A)
        score = sb("score", [P, NT, NE], f32, A)
        score2 = sb("score2", [P, NT, NE], f32, A)
        weigh = sb("weigh", [P, NT, NE], f32, A)
        first_of = sb("first_of", [P, NE], f32, A)
        sel = sb("sel", [P, NR, NT, NE], bf16, A)
        tmax = sb("tmax", [P, NR, NT], f32, A)
        tpick = sb("tpick", [P, NR, NT], f32, A)
        tsum = sb("tsum", [P, NT], f32, A)
        trec = sb("trec", [P, NT], f32, A)
        count_e = sb("count_e", [P, NE, NC], f32, A)
        scan_e = sb("scan_e", [P, NE, NC], f32, A)
        keep_going = sb("keep_going", [P, NE, NC], f32, A)
        place = sb("place", [P, NR, NT, NE], f32, A)
        loc = sb("loc", [P, NC], f32, A)
        kept = sb("kept", [P, NC], f32, A)
        pos = sb("pos", [P, NC], f32, A)
        hi_i = sb("hi_i", [P, NC], i32, A)
        slot_hi = sb("slot_hi", [P, NC], f32, A)
        slot_lo = sb("slot_lo", [P, NC], f32, A)
        col_no = sb("col_no", [P, NC], f32, A)
        oh_lo = sb("oh_lo", [P, 4, P], bf16, A)
        oh_hi = sb("oh_hi", [P, 4, 2, NS], bf16, A)
        sid = sb("sid", [P, NS], f32, A)
        empty = sb("empty", [P, NS], f32, A)
        above = sb("above", [P, NS], f32, A)
        trash = sb("trash", [P, NS // 4, 4], f32, A)
        attn_top = nc.sbuf_bytes_remaining
        A.close()

        M = only_moe
        w1_hi, w1_lo = sb("w1_hi", [P, 2, DC, HID], f32r, M), sb("w1_lo", [P, 2, DC, HID], f32r, M)
        w2_hi, w2_lo = sb("w2_hi", [P, 2, HJ, D], f32r, M), sb("w2_lo", [P, 2, HJ, D], f32r, M)
        xg = sb("xg", [P, 2, 2, D], f32, M)
        xT_hi, xT_lo = sb("xT_hi", [P, 2, DC, 2 * P], f32r, M), sb("xT_lo", [P, 2, DC, 2 * P], f32r, M)
        hraw = sb("hraw", [P, 4, 2, 2 * P], f32, M)
        h_hi, h_lo = sb("h_hi", [P, 2, HJ, 2 * P], f32r, M), sb("h_lo", [P, 2, HJ, 2 * P], f32r, M)
        y_sb = sb("y_sb", [P, 2, 2, D], f32, M)
        b2_sb = sb("b2_sb", [P, NE, D], f32, M)
        gate_s = sb("gate_s", [P, 2 * SPE, 2], f32, M)
        M.close()
        C = ExitStack()
        GT = 2
        NG = NT // GT
        RING = 4
        res = sb("res", [P, NT, D], f32, C)
        z = sb("z", [P, NT, D], f32, C)
        st_d, mv_d = sb("st_d", [P, RING, GT, 6], f32, C), sb("mv_d", [P, RING, GT, 2], f32, C)
        var_d, rstd_d, nmr_d = (sb(n, [P, RING, GT], f32, C) for n in ("var_d", "rstd_d", "nmr_d"))
        C.close()

        banks = root.enter_context(nc.psum_tensor("banks", [P, 8, 512], f32))
        PT, PV, TR, PJ = 4, 5, 6, 7
        XT, YB = 4, 5

        for name in (
            "load_small load_wq load_wkv load_wo load_ctx load_wg load_b1 load_b2 load_gb load_w1 load_w2 trash_zeroed gates_stored "
            "cleared half_made ident_made masks_made wg_cleared zero_made v_ones_made k_lo_made route_consts "
            "rstd1_made x_biased rstd2_made b1_copied w_lo_made beta_added rstd3_made z_scaled "
            "kT_made xn1T_hi_made q_hi_made pT_made probs_made valsT_hi_made xn2T_made logits_made router_exp "
            "xT_hi_made h_made y_scaled w_hi_made z_made "
            "kT_done v_done v_rows_done xn1T_done q_done scores_done pT_done pv_done valsT_done out_done "
            "xn2T_done logits_done counted placed rows_transposed fc1_done fc2_done "
            "kT_split v_made v_placed k_hi_made wq_split wo_split st1_made mv1_made var1_made xn1_made "
            "xn1T_lo_made q_lo_made max_made shifted rden_made vals_made valsT_lo_made x2_made st2_made mv2_made "
            "var2_made xn2_made router_shifted sel_made routed gates_made onehot_made ids_made xT_lo_made "
            "h_hi_made h_lo_made y_made st3_made mv3_made var3_made nmr_made out_made"
        ).split():
            sems[name] = root.enter_context(nc.semaphore(name))

        def sem(name):
            return sems[name]

        def dma_sem(name):
            return root.enter_context(nc.semaphore(name))

        load_x = [dma_sem(f"load_x{i}") for i in range(4)]
        load_small, load_wq, load_wkv, load_wo = sem("load_small"), sem("load_wq"), sem("load_wkv"), sem("load_wo")
        load_ctx, load_wg, load_b1, load_b2 = sem("load_ctx"), sem("load_wg"), sem("load_b1"), sem("load_b2")
        load_gb, load_w1, load_w2 = sem("load_gb"), sem("load_w1"), sem("load_w2")
        xn_stored = [dma_sem(f"xn_stored{u}") for u in range(2)]
        gathered = [dma_sem(f"gathered{u}") for u in range(2)]
        scattered = [dma_sem(f"scattered{u}") for u in range(2)]
        load_gate = [dma_sem(f"load_gate{u}") for u in range(2)]
        load_res = [dma_sem(f"load_res{u}") for u in range(RING)]
        stored = dma_sem("stored")

        block = root.enter_context(nc.Block())

        def attention_steps(engine, step):
            for i in (0, 1, 2):
                step(i, 0)
                step(i, 1)
            with engine.Fori(3, PAIRS - 2) as i:
                step(i, 0)
                step(i, 1)
            for i in (PAIRS - 2, PAIRS - 1, PAIRS):
                step(i, 0)
                step(i, 1)
            step(PAIRS + 1, 0)

        def expert_steps(engine, step):
            for c in range(SPE):
                step(0, c)
            with engine.Fori(0, 3) as g:
                for c in range(SPE, 3 * SPE):
                    step(g, c)
            for c in range(7 * SPE, NST + 3):
                step(0, c)

        def combine_steps(engine, step):
            for c in range(RING):
                step(0, c)
            with engine.Fori(1, NG // RING) as j:
                for c in range(RING):
                    step(j, c)
            for c in range(3):
                step(NG // RING, c)

        def batch_of(t):
            if isinstance(t, int):
                return t // TPB
            return nc.s_assert_within(t >> 3, 0, NB - 1,
                                      skip_runtime_bounds_check_because="t is a token tile of the loop, below 32")

        def within_st(g, c):
            return not isinstance(g, int) or 0 <= 10 * g + c < NST

        def w_parts(par, n):
            if n < 2:
                return w1_hi[:, par, n, :], w1_lo[:, par, n, :], w1raw[:, n, :]
            j = slice(4 * (n - 2), 4 * (n - 1))
            return w2_hi[:, par, j, :], w2_lo[:, par, j, :], w2raw[:, j, :]

        @block.sync
        def _(sp):
            sp.dma_start(ctx_sb[:], ctxT.rearrange("(c p) b k -> p c (b k)", p=P)).then_inc(load_ctx, 16)
            sp.dma_start(wk_sb[:], wkT.rearrange("(c p) o -> p c o", p=P)).then_inc(load_wkv, 16)
            sp.dma_start(X[:, 0:4, :], x_t[:, 0:4, :]).then_inc(load_x[0], 16)
            sp.dma_start(wv_sb[:], wvT.rearrange("(c p) o -> p c o", p=P)).then_inc(load_wkv, 16)
            sp.dma_start(wq_sb[:], wqT.rearrange("(c p) o -> p c o", p=P)).then_inc(load_wq, 16)
            for n, (a, b) in enumerate(((4, 12), (12, 22), (22, NT))):
                sp.dma_start(X[:, a:b, :], x_t[:, a:b, :]).then_inc(load_x[n + 1], 16)
            sp.dma_start(wo_sb[:], woT.rearrange("(c p) o -> p c o", p=P)).then_inc(load_wo, 16)
            sp.dma_start(w1raw[:], w1T[0].rearrange("(c p) h -> p c h", p=P)).then_inc(load_w1, 16)
            sp.dma_start(w2raw[:], w2[0].rearrange("(j p) d -> p j d", p=P)).then_inc(load_w2, 16)
            sp.wait_ge(sem("zero_made"), 1)
            sp.dma_start(sum_rows[N:N + 4 * P, :].rearrange("(q p) d -> p q d", p=P),
                         zero_row[:].unsqueeze(1).to_broadcast([P, 4, D])).then_inc(sem("trash_zeroed"), 16)
            sp.dma_start(gamma_sb[:], row(gamma)).then_inc(load_gb, 16)
            sp.dma_start(beta_sb[:], row(beta)).then_inc(load_gb, 16)

            def store_xn(i, u):
                if within(2 * i + u - 3, NT):
                    sp.wait_ge(sem("xn2_made"), 2 * i + u - 2)
                    for rows in (xn_t, sum_t):
                        sp.dma_start(rows[:, ds(2 * i + u - 3, 1), :].rearrange("p a d -> p (a d)"),
                                     xn2[:, 1 - u, :]).then_inc(xn_stored[1 - u], 16)

            attention_steps(sp, store_xn)
            sp.wait_ge(sem("gates_made"), 1)
            sp.dma_start(gate_rows.rearrange("(p c) a -> p (c a)", p=P), gates[:].rearrange("p r t -> p (r t)"))\
                .then_inc(sem("gates_stored"), 16)
            sp.wait_ge(sem("ids_made"), 2)
            sp.dma_start(b2_sb[:], b2.rearrange("(a e) d -> a e d", a=1).to_broadcast([P, NE, D])).then_inc(load_b2, 16)
            with sp.Fori(1, NE) as e:
                sp.wait_ge(sem("w_hi_made"), 4 * e - 2)
                sp.wait_ge(sem("w_lo_made"), 4 * e - 2)
                sp.dma_start(w1raw[:], w1T[ds(e, 1)].rearrange("a (c p) h -> p (a c) h", p=P)).then_inc(load_w1, 16)
                sp.wait_ge(sem("w_hi_made"), 4 * e)
                sp.wait_ge(sem("w_lo_made"), 4 * e)
                sp.dma_start(w2raw[:], w2[ds(e, 1)].rearrange("a (j p) d -> p (a j) d", p=P)).then_inc(load_w2, 16)
            sp.wait_ge(scattered[0], 32 * (NST // 2))
            sp.wait_ge(scattered[1], 32 * (NST // 2))

            for g in range(NG + 6):
                if within(g, NG):
                    c, t = g % RING, slice(g * GT, (g + 1) * GT)
                    wait(sp, load_res[c], 16 * (g // RING))
                    sp.dma_start(res[:, t, :], sum_t[:, t, :]).then_inc(load_res[c], 16)
                if within(g - 6, NG):
                    t = slice((g - 6) * GT, (g - 5) * GT)
                    sp.wait_ge(sem("out_made"), g - 5)
                    sp.dma_start(out_t[:, t, :], z[:, t, :]).then_inc(stored, 16)
            sp.wait_ge(stored, 16 * NG)

        @block.gpsimd
        def _(pool):
            g = nc.gpsimd
            g.memset(ident[:], 0.0).then_inc(sem("cleared"), 1)
            g.memset(key_of_row[:], 0.0).then_inc(sem("cleared"), 1)
            g.memset(head_of_feature[:], 1.0).then_inc(sem("cleared"), 1)
            g.memset(head_of_row[:], 1.0).then_inc(sem("cleared"), 1)
            g.memset(minus_half[:], -0.5).then_inc(sem("half_made"), 1)
            pool.wait_ge(sem("cleared"), 4)
            g.affine_select(out=ident[:], in_=ident[:], compare_op=ALU.not_equal, fill=1.0, base=0,
                            pattern=[[-1, P]], channel_multiplier=1).then_inc(sem("ident_made"), 1)
            g.affine_select(out=key_of_row[:], in_=key_of_row[:], compare_op=ALU.not_equal, fill=1.0, base=0,
                            pattern=[[0, HH], [-1, NK]], channel_multiplier=1).then_inc(sem("masks_made"), 1)
            g.affine_select(out=head_of_feature[:], in_=head_of_feature[:], compare_op=ALU.is_ge, fill=0.0, base=0,
                            pattern=[[-DH, HH]], channel_multiplier=1).then_inc(sem("cleared"), 1)
            g.affine_select(out=head_of_row[:], in_=head_of_row[:], compare_op=ALU.is_ge, fill=0.0, base=0,
                            pattern=[[JS, NJ], [-NK, HH]], channel_multiplier=1).then_inc(sem("cleared"), 1)
            pool.wait_ge(sem("cleared"), 6)
            g.affine_select(out=head_of_feature[:], in_=head_of_feature[:], compare_op=ALU.is_ge, fill=0.0,
                            base=DH - 1, pattern=[[DH, HH]], channel_multiplier=-1).then_inc(sem("masks_made"), 1)
            g.affine_select(out=head_of_row[:], in_=head_of_row[:], compare_op=ALU.is_ge, fill=0.0,
                            base=NK - 1, pattern=[[-JS, NJ], [NK, HH]], channel_multiplier=-1).then_inc(sem("cleared"), 1)
            pool.wait_ge(sem("cleared"), 7)
            g.memset(head_of_row[0:1, 1:NJ, :], 0.0).then_inc(sem("masks_made"), 1)
            g.memset(wg_sb[:], 0.0).then_inc(sem("wg_cleared"), 1)
            g.memset(zero_row[:], 0.0).then_inc(sem("zero_made"), 1)
            pool.wait_ge(sem("masks_made"), 3)
            vb = VB[:].rearrange("r (b f j w) -> r (b f) j w", f=2, j=NJ, w=VW)
            for bf in range(2 * NB):
                g.tensor_copy(vb[:, bf, :, P:VW], head_of_row[:]).then_inc(sem("v_ones_made"), 1)

            def rstd_first(j):
                if within(j, PAIRS):
                    pool.wait_ge(sem("var1_made"), j + 1)
                    g.tensor_tensor(rstd1[:], var1[:], minus_half[:, 0:2], ALU.pow).then_inc(sem("rstd1_made"), 1)

            rstd_first(0)
            pool.wait_ge(sem("kT_split"), 2 * DC)
            for f in range(DC):
                for b in range(NB):
                    g.tensor_tensor(KH_lo[:, (b * 2 + f) * KH:(b * 2 + f + 1) * KH].rearrange("p (h k) -> p h k", k=NK),
                                    kT_lo[:, f, b * NK:(b + 1) * NK].unsqueeze(1).to_broadcast([P, HH, NK]),
                                    head_of_feature[:].unsqueeze(2).to_broadcast([P, HH, NK]),
                                    ALU.mult).then_inc(sem("k_lo_made"), 1)
            g.memset(ones_bf[:], 1.0).then_inc(sem("route_consts"), 1)
            g.memset(upper[:], 1.0).then_inc(sem("cleared"), 1)
            g.memset(keep_going[:], 1.0).then_inc(sem("cleared"), 1)
            pool.wait_ge(sem("cleared"), 9)
            g.affine_select(out=upper[:], in_=upper[:], compare_op=ALU.is_ge, fill=0.0, base=0,
                            pattern=[[1, P]], channel_multiplier=-1).then_inc(sem("route_consts"), 1)
            g.memset(keep_going[:, :, 0:1], 0.0).then_inc(sem("route_consts"), 1)
            g.iota(iota_lo[:], pattern=[[1, P]], base=0, channel_multiplier=0,
                   allow_small_or_imprecise_dtypes=True).then_inc(sem("route_consts"), 1)
            g.iota(iota_hi[:], pattern=[[1, NS]], base=0, channel_multiplier=0,
                   allow_small_or_imprecise_dtypes=True).then_inc(sem("route_consts"), 1)
            g.iota(my_row[:], pattern=[[1, 1]], base=0, channel_multiplier=1,
                   allow_small_or_imprecise_dtypes=True).then_inc(sem("route_consts"), 1)
            g.iota(trash[:], pattern=[[0, NS // 4], [P, 4]], base=N + P, channel_multiplier=1,
                   allow_small_or_imprecise_dtypes=True).then_inc(sem("route_consts"), 1)
            g.iota(col_no[:], pattern=[[1, NC]], base=1, channel_multiplier=0,
                   allow_small_or_imprecise_dtypes=True).then_inc(sem("route_consts"), 1)
            g.iota(first_of[:], pattern=[[-1, NE]], base=NE, channel_multiplier=0,
                   allow_small_or_imprecise_dtypes=True).then_inc(sem("route_consts"), 1)

            def bias(j):
                if within(j, PAIRS):
                    pool.wait_ge(sem("xn1_made"), 2 * j + 2)
                    for v in range(2):
                        xt = X[:, ds(2 * j + v, 1), :].rearrange("p a d -> p (a d)")
                        g.tensor_tensor(xt, xt, bo_sb[:], ALU.add).then_inc(sem("x_biased"), 1)

            rstd_first(1)
            pool.wait_ge(load_small, 16 * 4)
            bias(0)

            def step(i, u):
                t = 2 * i + u
                if within(t - 2, NT):
                    pool.wait_ge(sem("var2_made"), t - 1)
                    g.tensor_tensor(rstd2[:, u:u + 1], var2[:, u:u + 1], minus_half[:, 0:1], ALU.pow)\
                        .then_inc(sem("rstd2_made"), 1)
                if u == 0:
                    bias(i + 1)
                else:
                    rstd_first(i + 2)

            attention_steps(pool, step)

            def gather(st):
                if within(st, NST):
                    u = st % 2
                    wait(pool, sem("rows_transposed"), st - 1)
                    for q in range(2):
                        g.indirect_dma_start(xg[:, u, q, :], None, xn_rows,
                                             bass.IndirectOffsetOnAxis(ap=slot_ids[:, st, 0, q:q + 1], axis=0),
                                             bounds_check=N - 1, oob_is_err=False).then_inc(gathered[u], 16)

            def gather_gates(st):
                if within(st, NST):
                    u, k = st % 2, st % (2 * SPE)
                    wait(pool, load_gate[u], 32 * (st // 2))
                    wait(pool, sem("y_scaled"), st + 1 - 2 * SPE)
                    for q in range(2):
                        g.indirect_dma_start(gate_s[:, k, q:q + 1], None, gate_rows,
                                             bass.IndirectOffsetOnAxis(ap=slot_ids[:, st, 2, q:q + 1], axis=0),
                                             bounds_check=P * NC - 1, oob_is_err=False).then_inc(load_gate[u], 16)

            def scatter(st):
                if within(st, NST):
                    u = st % 2
                    wait(pool, scattered[1 - u], 32 * ((st + 1) // 2))
                    pool.wait_ge(sem("y_scaled"), st + 1)
                    for q in range(2):
                        g.indirect_dma_start(sum_rows, bass.IndirectOffsetOnAxis(ap=slot_ids[:, st, 1, q:q + 1], axis=0),
                                             y_sb[:, u, q, :], None, bounds_check=N + 4 * P - 1, oob_is_err=False,
                                             compute_op=ALU.add).then_inc(scattered[u], 16)

            def split_quarter(e, n):
                par = e % 2
                wait(pool, sem("fc2_done"), SPE * (e - 1))
                wait(pool, load_w1 if n < 2 else load_w2, 16 * (e + 1))
                pool.wait_ge(sem("w_hi_made"), 4 * e + n + 1)
                if n == 0:
                    g.tensor_copy(b1_now[:, par, :], b1_sb[:, e * HJ:(e + 1) * HJ]).then_inc(sem("b1_copied"), 1)
                hi, lo, raw = w_parts(par, n)
                g.tensor_tensor(lo, raw, hi.bitcast(f32), ALU.subtract).then_inc(sem("w_lo_made"), 1)

            pool.wait_ge(sem("ids_made"), 2)
            for u in range(2):
                pool.wait_ge(xn_stored[u], 32 * PAIRS)
            gather(0)
            gather(1)
            pool.wait_ge(load_b1, 16)
            for n in range(4):
                split_quarter(0, n)
            pool.wait_ge(load_gb, 32)
            pool.wait_ge(sem("trash_zeroed"), 16)
            pool.wait_ge(sem("gates_stored"), 16)
            gather_gates(0)

            for st in range(NST + 2):
                gather(st + 2)
                gather_gates(st + 1)
                scatter(st - 2)
                if st < NT:
                    g.tensor_tensor(X[:, st, :], X[:, st, :], beta_sb[:], ALU.add).then_inc(sem("beta_added"), 1)
                e, quarter = st // SPE + 1, st % SPE - 1
                if quarter >= 0 and within(e, NE):
                    split_quarter(e, quarter)

            def combine(j, c):
                s = RING * j + c
                if within(s, NG):
                    pool.wait_ge(sem("var3_made"), s + 1)
                    g.tensor_tensor(rstd_d[:, c, :], var_d[:, c, :], minus_half[:, 0:GT], ALU.pow)\
                        .then_inc(sem("rstd3_made"), 1)
                if within(s - 2, NG):
                    for q in range(GT):
                        pool.wait_ge(sem("z_made"), GT * (s - 2) + q + 1)
                        zt = z[:, ds((s - 2) * GT + q, 1), :].rearrange("p a d -> p (a d)")
                        g.tensor_tensor(zt, zt, gamma_sb[:], ALU.mult).then_inc(sem("z_scaled"), 1)

            combine_steps(pool, combine)

        @block.scalar
        def _(act):
            a = nc.scalar
            act.dma_start(bq_sb[:], bq).then_inc(load_small, 16)
            act.dma_start(bk_sb[:], bk).then_inc(load_small, 16)
            act.dma_start(bv_sb[:], row(bv)).then_inc(load_small, 16)
            act.dma_start(bo_sb[:], row(bo)).then_inc(load_small, 16)
            act.dma_start(b1_sb[:], b1T).then_inc(load_b1, 16)
            act.wait_ge(sem("wg_cleared"), 1)
            act.dma_start(wg_sb[:, :, 0:NE], wg.rearrange("(c p) e -> p c e", p=P)).then_inc(load_wg, 16)
            act.wait_ge(load_small, 16 * 4)
            for f in range(DC):
                act.wait_ge(sem("kT_done"), f + 1)
                a.activation(kT[:, f, :], banks[:, f, 0:NB * NK], ACT.Identity, bias=bk_sb[:, f:f + 1])\
                    .then_inc(sem("kT_made"), 1)

            def first_layernorm(j):
                if within(j, PAIRS):
                    act.wait_ge(sem("xn1T_done"), j + 1)
                    a.activation(xn1T_hi[:].rearrange("p c t -> p (c t)"), banks[:, TR, :], ACT.Copy)\
                        .then_inc(sem("xn1T_hi_made"), 1)

            def queries(j):
                if within(j, PAIRS):
                    act.wait_ge(sem("q_done"), j + 1)
                    for f in range(DC):
                        a.activation(q_hi[:, f, :], banks[:, PJ, f * 256:(f + 1) * 256], ACT.Identity,
                                     bias=bq_sb[:, f:f + 1]).then_inc(sem("q_hi_made"), 1)

            first_layernorm(0)
            queries(0)

            def step(i, u):
                t = 2 * i + u

                def probs_transposed(n):
                    if within(t - 1, NT):
                        f, w = n // 2, (3, 2)[n % 2]
                        j0 = NJ * f + 3 * (n % 2)
                        act.wait_ge(sem("pT_done"), 4 * (t - 1) + n + 1)
                        a.activation(probsT[:, j0:j0 + w, :].rearrange("r j q -> r (j q)"),
                                     banks[0:JW, PT, 0:w * P], ACT.Copy).then_inc(sem("pT_made"), 1)

                def exp(f):
                    if within(t, NT):
                        act.wait_ge(sem("shifted"), 2 * t + f + 1)
                        e = probs[:, u, f * KH:(f + 1) * KH]
                        a.activation(e, e, ACT.Exp, scale=SCALE).then_inc(sem("probs_made"), 1)

                probs_transposed(0)
                if within(t - 2, NT):
                    act.wait_ge(sem("valsT_done"), t - 1)
                    a.activation(valsT_hi[:].rearrange("p c q -> p (c q)"), banks[:, TR, 0:256], ACT.Copy)\
                        .then_inc(sem("valsT_hi_made"), 1)
                probs_transposed(1)
                exp(0)
                probs_transposed(2)
                if within(t - 3, NT):
                    act.wait_ge(sem("xn2T_done"), t - 2)
                    a.activation(xn2T[:].rearrange("p c q -> p (c q)"), banks[:, TR, 256:512], ACT.Copy)\
                        .then_inc(sem("xn2T_made"), 1)
                probs_transposed(3)
                exp(1)
                if within(t - 3, NT):
                    done = in_register(act, t - 2)
                    act.wait_ge(load_wg, 16)
                    act.wait_ge(sem("logits_done"), done)
                    a.activation(logits[:, ds(t - 3, 1), :].rearrange("p a e -> p (a e)"), banks[:, PJ, 256:256 + NE],
                                 ACT.Copy).then_inc(sem("logits_made"), 1)
                if u == 0:
                    first_layernorm(i + 1)
                else:
                    queries(i + 1)

            attention_steps(act, step)

            act.wait_ge(sem("router_shifted"), 1)
            a.activation(score[:], score[:], ACT.Exp).then_inc(sem("router_exp"), 1)

            def split_quarter(e, par, n):
                wait(act, sem("fc2_done"), SPE * (e - 1))
                wait(act, load_w1 if n < 2 else load_w2, 16 * (e + 1))
                hi, lo, raw = w_parts(par, n)
                a.activation(hi, raw, ACT.Copy).then_inc(sem("w_hi_made"), 1)

            def rows_hi(gq, c):
                if within_st(gq, c):
                    act.wait_ge(sem("rows_transposed"), 10 * gq + c + 1)
                    a.activation(xT_hi[:, c % 2].rearrange("p c t -> p (c t)"), banks[:, XT, :], ACT.Copy)\
                        .then_inc(sem("xT_hi_made"), 1)

            act.wait_ge(sem("ids_made"), 2)
            act.wait_ge(load_b1, 16)
            for n in range(4):
                split_quarter(0, 0, n)
            rows_hi(0, 0)

            def scale_results(gq, c):
                if within_st(gq, c):
                    act.wait_ge(load_gate[c % 2], 32 * (5 * gq + c // 2 + 1))
                    act.wait_ge(sem("y_made"), 10 * gq + c + 1)
                    for q in range(2):
                        y = y_sb[:, c % 2, q, :]
                        m = a.activation(y, y, ACT.Copy, scale=gate_s[:, c % (2 * SPE), q:q + 1])
                    m.then_inc(sem("y_scaled"), 1)

            def expert_step(gq, c):
                rows_hi(gq, c + 1)
                if within_st(gq, c):
                    st = 10 * gq + c
                    for j in range(HJ):
                        if j % 2 == 0:
                            wait(act, sem("h_lo_made"), 4 * (st - 1) + j // 2 + 1)
                            act.wait_ge(sem("fc1_done"), 4 * st + j // 2 + 1)
                        a.activation(hraw[:, j // 2, j % 2, :], banks[:, j // 2, (j % 2) * 256:(j % 2 + 1) * 256],
                                     ACT.Silu, bias=b1_now[:, (c // SPE) % 2, j:j + 1])\
                            .then_inc(sem("h_made"), 1)
                scale_results(gq, c - 2)
                e, s = 2 * gq + c // SPE + 1, c % SPE
                if s and within(e, NE):
                    split_quarter(e, (c // SPE + 1) % 2, s - 1)

            expert_steps(act, expert_step)

            def combine(j, c):
                s = RING * j + c
                if within(s - 1, NG):
                    act.wait_ge(sem("nmr_made"), s)
                    for q in range(GT):
                        t, r = ds((s - 1) * GT + q, 1), (c - 1) % RING
                        a.activation(z[:, t, :].rearrange("p a d -> p (a d)"), res[:, t, :].rearrange("p a d -> p (a d)"),
                                     ACT.Identity, scale=rstd_d[:, r, q:q + 1], bias=nmr_d[:, r, q:q + 1])\
                            .then_inc(sem("z_made"), 1)

            combine_steps(act, combine)

        @block.tensor
        def _(pe):
            t_ = nc.tensor

            def mm3(o, a_hi, a_lo, b_hi, b_lo, first, last):
                t_.matmul(o, a_hi, b_hi, start=first, stop=False)
                t_.matmul(o, a_hi, b_lo, start=False, stop=False)
                return t_.matmul(o, a_lo, b_hi, start=False, stop=last)

            pe.wait_ge(load_ctx, 16)
            pe.wait_ge(load_wkv, 32)
            for f in range(DC):
                for c in range(DC):
                    m = t_.matmul(banks[:, f, 0:NB * NK], wk_sb[:, c, f * P:(f + 1) * P], ctx_sb[:, c, :],
                                  start=(c == 0), stop=(c == DC - 1))
                m.then_inc(sem("kT_done"), 1)
            for b in range(NB):
                for c in range(DC):
                    m = t_.matmul(banks[0:NK, 2 + b // 2, (b % 2) * D:(b % 2 + 1) * D],
                                  ctx_sb[:, c, b * NK:(b + 1) * NK], wv_sb[:, c, :], start=(c == 0), stop=(c == DC - 1))
                m.then_inc(sem("v_done"), 1)
            pe.wait_ge(sem("masks_made"), 3)
            rows = key_of_row[:].rearrange("k h r -> k (h r)")
            for n in range(NB * NJ):
                b, j = divmod(n, NJ)
                if j == 0:
                    pe.wait_ge(sem("v_made"), b + 1)
                wait(pe, sem("v_placed"), n - 3)
                t_.matmul(banks[0:JW, 4 + n % 4, 0:D], rows[:, j * JS:j * JS + JW], v_sb[:, b, :],
                          start=True, stop=True).then_inc(sem("v_rows_done"), 1)
            pe.wait_ge(sem("v_placed"), NB * NJ)
            pe.wait_ge(sem("ident_made"), 1)

            def first_layernorm(j):
                if within(j, PAIRS):
                    pe.wait_ge(sem("xn1_made"), 2 * j + 2)
                    for v in range(2):
                        for c in range(DC):
                            m = t_.transpose(banks[:, TR, c * 256 + v * P:c * 256 + (v + 1) * P],
                                             xn1[:, v, c * P:(c + 1) * P], ident[:])
                    m.then_inc(sem("xn1T_done"), 1)

            def queries(j):
                if within(j, PAIRS):
                    pe.wait_ge(sem("xn1T_hi_made"), j + 1)
                    pe.wait_ge(sem("xn1T_lo_made"), j + 1)
                    for f in range(DC):
                        for c in range(DC):
                            fs = slice(f * P, (f + 1) * P)
                            m = mm3(banks[:, PJ, f * 256:(f + 1) * 256], wq_hi[:, c, fs], wq_lo[:, c, fs],
                                    xn1T_hi[:, c, :], xn1T_lo[:, c, :], c == 0, c == DC - 1)
                    m.then_inc(sem("q_done"), 1)

            first_layernorm(0)
            pe.wait_ge(sem("wq_split"), 2)
            queries(0)
            pe.wait_ge(sem("k_hi_made"), 2 * NB)
            pe.wait_ge(sem("k_lo_made"), 2 * NB)
            pe.wait_ge(sem("wo_split"), 2)
            pe.wait_ge(load_wg, 16)
            pe.wait_ge(sem("v_ones_made"), 2 * NB)

            def step(i, u):
                t = 2 * i + u

                def scores(f):
                    if within(t, NT):
                        b = batch_of(t)
                        pe.wait_ge(sem("q_hi_made"), DC * (i + 1))
                        pe.wait_ge(sem("q_lo_made"), DC * (i + 1))
                        wait(pe, sem("shifted"), 2 * (t - 1) + f + 1)
                        for h in range(2):
                            ks = ds((2 * b + f) * KH + h * KC, KC)
                            m = mm3(banks[:, 2 * f + h, 0:KC], q_hi[:, f, u * P:(u + 1) * P],
                                    q_lo[:, f, u * P:(u + 1) * P], KH_hi[:, ks], KH_lo[:, ks], True, True)
                        m.then_inc(sem("scores_done"), 1)

                def transpose_probs(n):
                    if within(t - 1, NT):
                        f = n // 2
                        j0, w = 3 * (n % 2), (3, 2)[n % 2]
                        pe.wait_ge(sem("probs_made"), 2 * (t - 1) + f + 1)
                        wait(pe, sem("pT_made"), 4 * (t - 1) + n)
                        for j in range(j0, j0 + w):
                            m = t_.transpose(banks[0:JW, PT, (j - j0) * P:(j - j0 + 1) * P],
                                             probs[:, 1 - u, f * KH + j * JS:f * KH + j * JS + JW], ident[:])
                        m.then_inc(sem("pT_done"), 1)

                def weigh_values(n):
                    if within(t - 1, NT):
                        b = batch_of(t - 1)
                        f = n // 2
                        j0, w = 3 * (n % 2), (3, 2)[n % 2]
                        if n == 0:
                            wait(pe, sem("vals_made"), t - 1)
                        pe.wait_ge(sem("pT_made"), 4 * (t - 1) + n + 1)
                        for j in range(j0, j0 + w):
                            m = t_.matmul(banks[:, PV, f * VW:(f + 1) * VW], probsT[:, NJ * f + j, :],
                                          VB[:, ds(((2 * b + f) * NJ + j) * VW, VW)],
                                          start=(j == 0), stop=(j == NJ - 1))
                        if n == 3:
                            m.then_inc(sem("pv_done"), 1)

                scores(0)
                scores(1)
                transpose_probs(0)
                if within(t - 2, NT):
                    pe.wait_ge(sem("vals_made"), t - 1)
                    wait(pe, sem("xn2T_made"), t - 3)
                    if u == 1:
                        first = i + 2
                        if within(i + 1, PAIRS):
                            pe.wait_ge(sem("xn1T_hi_made"), first)
                            pe.wait_ge(sem("xn1T_lo_made"), first)
                    for c in range(DC):
                        m = t_.transpose(banks[:, TR, c * P:(c + 1) * P], vals[:, c * P:(c + 1) * P], ident[:])
                    m.then_inc(sem("valsT_done"), 1)
                transpose_probs(1)
                weigh_values(0)
                if within(t - 2, NT):
                    pe.wait_ge(sem("valsT_hi_made"), t - 1)
                    pe.wait_ge(sem("valsT_lo_made"), t - 1)
                    wait(pe, sem("logits_made"), t - 3)
                    if u == 0 and within(i, PAIRS):
                        pe.wait_ge(sem("q_hi_made"), DC * (i + 1))
                        pe.wait_ge(sem("q_lo_made"), DC * (i + 1))
                    for c in range(DC):
                        m = mm3(banks[:, PJ, 0:D], valsT_hi[:, c, :], valsT_lo[:, c, :], wo_hi[:, c, :], wo_lo[:, c, :],
                                c == 0, c == DC - 1)
                    m.then_inc(sem("out_done"), 1)
                transpose_probs(2)
                weigh_values(1)
                if within(t - 3, NT):
                    pe.wait_ge(sem("xn2_made"), t - 2)
                    if within(t - 2, NT):
                        pe.wait_ge(sem("valsT_hi_made"), t - 1)
                        pe.wait_ge(sem("valsT_lo_made"), t - 1)
                    for c in range(DC):
                        m = t_.transpose(banks[:, TR, 256 + c * P:256 + (c + 1) * P],
                                         xn2[:, 1 - u, c * P:(c + 1) * P], ident[:])
                    m.then_inc(sem("xn2T_done"), 1)
                transpose_probs(3)
                weigh_values(2)
                if within(t - 3, NT):
                    pe.wait_ge(sem("xn2T_made"), t - 2)
                    if within(t - 2, NT):
                        pe.wait_ge(sem("x2_made"), t - 1)
                    for c in range(DC):
                        m = t_.matmul(banks[:, PJ, 256:256 + P], xn2T[:, c, :], wg_sb[:, c, :],
                                      start=(c == 0), stop=(c == DC - 1))
                    m.then_inc(sem("logits_done"), 1)
                weigh_values(3)
                if u == 0:
                    if within(i + 1, PAIRS):
                        wait(pe, sem("xn2T_made"), t - 2)
                        if within(t - 2, NT):
                            pe.wait_ge(sem("valsT_hi_made"), t - 1)
                            pe.wait_ge(sem("valsT_lo_made"), t - 1)
                    first_layernorm(i + 1)
                else:
                    if within(i + 1, PAIRS):
                        wait(pe, sem("logits_made"), t - 2)
                        if within(t - 2, NT):
                            pe.wait_ge(sem("x2_made"), t - 1)
                    queries(i + 1)

            attention_steps(pe, step)

            pe.wait_ge(sem("route_consts"), 9)
            pe.wait_ge(sem("sel_made"), 2)
            flat = sel[:].rearrange("p r t e -> p (r t e)")
            t_.matmul(banks[:, 0, :], ones_bf[:], flat, start=True, stop=True).then_inc(sem("counted"), 1)
            t_.matmul(banks[:, 1, :], upper[:], flat, start=True, stop=True).then_inc(sem("counted"), 1)
            for n in range(NC):
                pe.wait_ge(sem("onehot_made"), n + 1)
                t_.matmul(banks[:, 2, 0:2 * NS], oh_lo[:, n % 4, :], oh_hi[:, n % 4].rearrange("p a s -> p (a s)"),
                          start=(n == 0), stop=(n == NC - 1)).then_inc(sem("placed"), 1)

            def transpose_rows(gq, c):
                if within_st(gq, c):
                    st = 10 * gq + c
                    n, u = 5 * gq + c // 2, c % 2
                    pe.wait_ge(gathered[u], 32 * (n + 1))
                    wait(pe, sem("xT_hi_made"), st)
                    wait(pe, sem("xT_lo_made"), st)
                    for q in range(2):
                        for k in range(DC):
                            m = t_.transpose(banks[:, XT, k * 256 + q * P:k * 256 + (q + 1) * P],
                                             xg[:, u, q, k * P:(k + 1) * P], ident[:])
                    m.then_inc(sem("rows_transposed"), 1)

            def fc1(gq, c):
                if within_st(gq, c):
                    st, u, w = 10 * gq + c, c % 2, (c // SPE) % 2
                    e = 2 * gq + c // SPE
                    pe.wait_ge(sem("xT_hi_made"), st + 1)
                    pe.wait_ge(sem("xT_lo_made"), st + 1)
                    pe.wait_ge(sem("w_hi_made"), 4 * e + 2)
                    pe.wait_ge(sem("w_lo_made"), 4 * e + 2)
                    for j in range(HJ):
                        if j % 2 == 0:
                            wait(pe, sem("h_made"), HJ * (st - 1) + j + 2)
                        hs = slice(j * P, (j + 1) * P)
                        for k in range(DC):
                            m = mm3(banks[:, j // 2, (j % 2) * 256:(j % 2 + 1) * 256], w1_hi[:, w, k, hs],
                                    w1_lo[:, w, k, hs], xT_hi[:, u, k, :], xT_lo[:, u, k, :], k == 0, k == DC - 1)
                        if j % 2:
                            m.then_inc(sem("fc1_done"), 1)

            def fc2(gq, c):
                if within_st(gq, c):
                    st, u, w = 10 * gq + c, c % 2, (c // SPE) % 2
                    e = 2 * gq + c // SPE
                    pe.wait_ge(sem("w_hi_made"), 4 * e + 4)
                    pe.wait_ge(sem("w_lo_made"), 4 * e + 4)
                    wait(pe, sem("y_made"), st - 1)
                    for q in range(2):
                        qs = slice(q * P, (q + 1) * P)
                        for j in range(HJ):
                            if q == 0 and j % 2 == 0:
                                pe.wait_ge(sem("h_lo_made"), 4 * st + j // 2 + 1)
                            m = mm3(banks[:, YB + u, q * D:(q + 1) * D], h_hi[:, u, j, qs], h_lo[:, u, j, qs],
                                    w2_hi[:, w, j, :], w2_lo[:, w, j, :], j == 0, j == HJ - 1)
                    m.then_inc(sem("fc2_done"), 1)

            transpose_rows(0, 0)

            def expert_step(gq, c):
                transpose_rows(gq, c + 1)
                fc1(gq, c)
                fc2(gq, c - 1)

            expert_steps(pe, expert_step)

        @block.vector
        def _(dve):
            v = nc.vector

            def split(hi, lo, raw, name):
                v.tensor_copy(hi[:], raw[:]).then_inc(sem(name), 1)
                dve.wait_ge(sem(name), 1)
                v.tensor_tensor(lo[:], raw[:], hi[:].bitcast(f32), ALU.subtract).then_inc(sem(name), 1)

            def stats_first(j):
                if within(j, PAIRS):
                    row_stats(j)
                    dve.wait_ge(sem("st1_made"), 2 * j + 2)
                    aggregate(j)

            def row_stats(j):
                if within(j, PAIRS):
                    for u in range(2):
                        v.bn_stats(st1[:, u, :], X[:, ds(2 * j + u, 1), :].rearrange("p a d -> p (a d)"))\
                            .then_inc(sem("st1_made"), 1)

            def aggregate(j):
                if within(j, PAIRS):
                    for u in range(2):
                        v.bn_aggr(mv1[:, u, :], st1[:, u, :]).then_inc(sem("mv1_made"), 1)
                    dve.wait_ge(sem("mv1_made"), 2 * j + 2)
                    wait(dve, sem("rstd1_made"), j)
                    v.tensor_scalar_add(var1[:], mv1[:, :, 1], EPS_LN).then_inc(sem("var1_made"), 1)

            def normalise_first(j):
                if within(j, PAIRS):
                    dve.wait_ge(sem("rstd1_made"), j + 1)
                    wait(dve, sem("xn1T_done"), j)
                    for u in range(2):
                        v.tensor_scalar(xn1[:, u, :], X[:, ds(2 * j + u, 1), :].rearrange("p a d -> p (a d)"),
                                        mv1[:, u, 0:1], rstd1[:, u:u + 1], ALU.subtract, ALU.mult)\
                            .then_inc(sem("xn1_made"), 1)

            def first_lo(j):
                if within(j, PAIRS):
                    dve.wait_ge(sem("xn1T_hi_made"), j + 1)
                    v.tensor_tensor(xn1T_lo[:].rearrange("p c t -> p (c t)"), banks[:, TR, :],
                                    xn1T_hi[:].rearrange("p c t -> p (c t)").bitcast(f32), ALU.subtract)\
                        .then_inc(sem("xn1T_lo_made"), 1)

            def queries_lo(j, stats_of=None):
                if within(j, PAIRS):
                    for f in range(DC):
                        if stats_of is not None and within(stats_of, PAIRS):
                            dve.wait_ge(sem("st1_made"), 2 * stats_of + 2)
                        dve.wait_ge(sem("q_hi_made"), DC * (j + 1))
                        v.scalar_tensor_tensor(q_lo[:, f, :], banks[:, PJ, f * 256:(f + 1) * 256], bq_sb[:, f:f + 1],
                                               q_hi[:, f, :].bitcast(f32), ALU.add, ALU.subtract)\
                            .then_inc(sem("q_lo_made"), 1)

            dve.wait_ge(load_small, 64)
            for f in range(DC):
                dve.wait_ge(sem("kT_made"), f + 1)
                v.tensor_copy(kT_hi[:, f, :], kT[:, f, :]).then_inc(sem("kT_split"), 1)
            for f in range(DC):
                dve.wait_ge(sem("kT_split"), DC)
                v.tensor_tensor(kT_lo[:, f, :], kT[:, f, :], kT_hi[:, f, :].bitcast(f32), ALU.subtract)\
                    .then_inc(sem("kT_split"), 1)
            for b in range(NB):
                dve.wait_ge(sem("v_done"), 2 * (b // 2) + 2)
                v.tensor_tensor(v_sb[:, b, :], banks[0:NK, 2 + b // 2, (b % 2) * D:(b % 2 + 1) * D], bv_sb[0:NK, :],
                                ALU.add).then_inc(sem("v_made"), 1)
            dve.wait_ge(load_x[0], 16)
            stats_first(0)
            normalise_first(0)
            stats_first(1)
            dve.wait_ge(load_wq, 16)
            split(wq_hi, wq_lo, wq_sb, "wq_split")
            dve.wait_ge(sem("masks_made"), 3)
            for n in range(NB * NJ):
                b, j = divmod(n, NJ)
                dve.wait_ge(sem("v_rows_done"), n + 1)
                v.tensor_tensor(VB[:].rearrange("r (b f j w) -> r b f j w", b=NB, f=2, j=NJ)[:, b, :, j, 0:P]
                                .rearrange("r f (h d) -> r f h d", d=DH),
                                banks[0:JW, 4 + n % 4, 0:D].rearrange("r (f h d) -> r f h d", f=2, d=DH),
                                head_of_row[:, j, :].unsqueeze(1).unsqueeze(3).to_broadcast([JW, 2, HH, DH]),
                                ALU.mult).then_inc(sem("v_placed"), 1)
            first_lo(0)
            for f in range(DC):
                for b in range(NB):
                    v.tensor_tensor(KH_hi[:, (b * 2 + f) * KH:(b * 2 + f + 1) * KH].rearrange("p (h k) -> p h k", k=NK),
                                    kT_hi[:, f, b * NK:(b + 1) * NK].bitcast(f32).unsqueeze(1)
                                    .to_broadcast([P, HH, NK]),
                                    head_of_feature[:].unsqueeze(2).to_broadcast([P, HH, NK]),
                                    ALU.mult).then_inc(sem("k_hi_made"), 1)
            queries_lo(0)
            dve.wait_ge(load_wo, 16)
            split(wo_hi, wo_lo, wo_sb, "wo_split")
            for n in range(1, 4):
                dve.wait_ge(load_x[n], 16)

            def step(i, u):
                t = 2 * i + u
                if within(t - 2, NT):
                    dve.wait_ge(sem("pv_done"), t - 1)
                    pv = banks[:, PV, 0:2 * VW].rearrange("p (f w) -> p f w", w=VW)
                    v.reciprocal(rden[:], pv[:, :, P:VW]).then_inc(sem("rden_made"), 1)
                    dve.wait_ge(sem("rden_made"), t - 1)
                    v.tensor_tensor(vals[:].rearrange("p (f h d) -> p f h d", f=2, d=DH),
                                    pv[:, :, 0:P].rearrange("p f (h d) -> p f h d", d=DH),
                                    rden[:].unsqueeze(3).to_broadcast([P, 2, HH, DH]),
                                    ALU.mult).then_inc(sem("vals_made"), 1)
                if within(t - 3, NT):
                    dve.wait_ge(sem("rstd2_made"), t - 2)
                    wait(dve, sem("xn2T_done"), t - 4)
                    wait(dve, xn_stored[1 - u], 32 * ((t - 3) // 2 if isinstance(t, int) else (t - 3) >> 1))
                    v.tensor_scalar(xn2[:, 1 - u, :], X[:, ds(t - 3, 1), :].rearrange("p a d -> p (a d)"),
                                    mv2[:, 1 - u, 0:1], rstd2[:, 1 - u:2 - u], ALU.subtract, ALU.mult)\
                        .then_inc(sem("xn2_made"), 1)
                if u == 0:
                    normalise_first(i + 1)

                def shift(f):
                    if within(t, NT):
                        s = banks[:, 2 * f:2 * f + 2, 0:KC].rearrange("p c (h k) -> p c h k", k=NK)
                        dve.wait_ge(sem("scores_done"), 2 * t + f + 1)
                        v.tensor_reduce(rowmax[:, f, :].rearrange("p (c h) -> p c h", c=2), s, AX, ALU.max)\
                            .then_inc(sem("max_made"), 1)
                        dve.wait_ge(sem("max_made"), 2 * t + f + 1)
                        wait(dve, sem("pT_made"), 4 * (t - 2) + 2 * f + 2)
                        v.tensor_tensor(probs[:, u, f * KH:(f + 1) * KH].rearrange("p (c h k) -> p c h k", c=2, k=NK),
                                        s, rowmax[:, f, :].rearrange("p (c h) -> p c h", c=2).unsqueeze(3)
                                        .to_broadcast([P, 2, HH // 2, NK]),
                                        ALU.subtract).then_inc(sem("shifted"), 1)

                shift(0)
                if within(t - 2, NT):
                    dve.wait_ge(sem("valsT_hi_made"), t - 1)
                    v.tensor_tensor(valsT_lo[:].rearrange("p c q -> p (c q)"), banks[:, TR, 0:256],
                                    valsT_hi[:].rearrange("p c q -> p (c q)").bitcast(f32), ALU.subtract)\
                        .then_inc(sem("valsT_lo_made"), 1)
                shift(1)
                if within(t - 2, NT):
                    dve.wait_ge(sem("out_done"), t - 1)
                    dve.wait_ge(sem("x_biased"), t - 1)
                    xt = X[:, ds(t - 2, 1), :].rearrange("p a d -> p (a d)")
                    v.tensor_tensor(xt, banks[:, PJ, 0:D], xt, ALU.add).then_inc(sem("x2_made"), 1)
                    dve.wait_ge(load_x[3], 16)
                    dve.wait_ge(sem("x2_made"), t - 1)
                    v.bn_stats(st2[:, u, :], xt).then_inc(sem("st2_made"), 1)
                    dve.wait_ge(load_x[3], 16)
                    dve.wait_ge(sem("st2_made"), t - 1)
                    v.bn_aggr(mv2[:, u, :], st2[:, u, :]).then_inc(sem("mv2_made"), 1)
                    dve.wait_ge(sem("mv2_made"), t - 1)
                    v.tensor_scalar_add(var2[:, u:u + 1], mv2[:, u, 1:2], EPS_LN).then_inc(sem("var2_made"), 1)
                if u == 0:
                    first_lo(i + 1)
                else:
                    row_stats(i + 2)
                    queries_lo(i + 1, stats_of=i + 2)
                    aggregate(i + 2)

            attention_steps(dve, step)

            done = [0]

            def then(ins):
                done[0] += 1
                ins.then_inc(sem("routed"), 1)
                dve.wait_ge(sem("routed"), done[0])

            def over_e(x2):
                return x2.unsqueeze(2).to_broadcast([P, NT, NE])

            dve.wait_ge(sem("logits_made"), NT)
            dve.wait_ge(sem("route_consts"), 9)
            then(v.tensor_reduce(tsum[:], logits[:], AX, ALU.max))
            v.tensor_tensor(score[:], logits[:], over_e(tsum[:]), ALU.subtract).then_inc(sem("router_shifted"), 1)
            dve.wait_ge(sem("router_exp"), 1)
            then(v.tensor_reduce(tsum[:], score[:], AX, ALU.add))
            then(v.reciprocal(trec[:], tsum[:]))
            then(v.tensor_tensor(score2[:], score[:], over_e(trec[:]), ALU.mult))
            for r in range(NR):
                then(v.tensor_reduce(tmax[:, r, :], score2[:], AX, ALU.max))
                then(v.tensor_tensor(weigh[:], score2[:], over_e(tmax[:, r, :]), ALU.is_equal))
                then(v.tensor_tensor(weigh[:], weigh[:], first_of[:].unsqueeze(1).to_broadcast([P, NT, NE]), ALU.mult))
                then(v.tensor_reduce(tpick[:, r, :], weigh[:], AX, ALU.max))
                v.tensor_tensor(sel[:, r], weigh[:], over_e(tpick[:, r, :]), ALU.is_equal).then_inc(sem("sel_made"), 1)
                if r == 0:
                    dve.wait_ge(sem("sel_made"), 1)
                    then(v.scalar_tensor_tensor(score2[:], sel[:, 0], -2.0, score2[:], ALU.mult, ALU.add))
            then(v.tensor_tensor(tsum[:], tmax[:, 0, :], tmax[:, 1, :], ALU.add))
            then(v.tensor_scalar_max(tsum[:], tsum[:], EPS_GATE))
            then(v.reciprocal(trec[:], tsum[:]))
            then(v.tensor_tensor(gates[:], tmax[:], trec[:].unsqueeze(1).to_broadcast([P, NR, NT]), ALU.mult))
            dve.wait_ge(sem("counted"), 2)
            then(v.tensor_copy(count_e[:].rearrange("p e c -> p c e"),
                               banks[:, 0, :].rearrange("p (c e) -> p c e", e=NE)))
            then(v.tensor_tensor_scan(scan_e[:].rearrange("p e c -> p (e c)"),
                                      keep_going[:].rearrange("p e c -> p (e c)"),
                                      count_e[:].rearrange("p e c -> p (e c)"), 0.0, ALU.mult, ALU.add))
            then(v.tensor_tensor(scan_e[:], scan_e[:], count_e[:], ALU.subtract))
            flat_place = place[:].rearrange("p r t e -> p (r t) e")
            then(v.tensor_tensor(flat_place, banks[:, 1, :].rearrange("p (c e) -> p c e", e=NE),
                                 scan_e[:].rearrange("p e c -> p c e"), ALU.add))
            then(v.tensor_tensor(flat_place, flat_place, sel[:].rearrange("p r t e -> p (r t) e"), ALU.mult))
            then(v.tensor_reduce(loc[:], flat_place, AX, ALU.add))
            then(v.tensor_scalar(kept[:], loc[:], float(CAP), None, ALU.is_le))
            pick = tpick[:].rearrange("p r t -> p (r t)")
            then(v.scalar_tensor_tensor(pos[:], pick, -float(CAP), loc[:], ALU.mult, ALU.add))
            then(v.tensor_scalar_add(pos[:], pos[:], float(NE * CAP - 1)))
            then(v.tensor_scalar(slot_lo[:], pos[:], -(P - 1) / 2.0, 1.0 / P, ALU.add, ALU.mult))
            then(v.tensor_copy(hi_i[:], slot_lo[:]))
            then(v.tensor_copy(slot_hi[:], hi_i[:]))
            then(v.scalar_tensor_tensor(slot_lo[:], slot_hi[:], -float(P), pos[:], ALU.mult, ALU.add))
            then(v.tensor_scalar_add(slot_hi[:], slot_hi[:], 1.0))
            then(v.tensor_tensor(slot_hi[:], slot_hi[:], kept[:], ALU.mult))
            then(v.tensor_scalar_add(slot_hi[:], slot_hi[:], -1.0))
            gflat = gates[:].rearrange("p r t -> p (r t)")
            v.tensor_tensor(gflat, gflat, kept[:], ALU.mult).then_inc(sem("gates_made"), 1)
            for n in range(NC):
                wait(dve, sem("placed"), n - 3)
                v.tensor_scalar(oh_lo[:, n % 4, :], iota_lo[:], slot_lo[:, n:n + 1], None, ALU.is_equal)
                v.tensor_scalar(oh_hi[:, n % 4, 0, :], iota_hi[:], slot_hi[:, n:n + 1], my_row[:, 0:1],
                                ALU.is_equal, ALU.mult)
                v.tensor_scalar(oh_hi[:, n % 4, 1, :], iota_hi[:], slot_hi[:, n:n + 1], col_no[:, n:n + 1],
                                ALU.is_equal, ALU.mult).then_inc(sem("onehot_made"), 1)
            dve.wait_ge(sem("placed"), NC)
            tab = banks[:, 2, 0:2 * NS]
            pair = "p (s q) -> p s q"
            then(v.tensor_copy(empty[:], tab[:, NS:2 * NS]))
            then(v.scalar_tensor_tensor(sid[:], tab[:, 0:NS], float(NC), empty[:], ALU.mult, ALU.add))
            then(v.tensor_scalar_add(sid[:], sid[:], -1.0))
            then(v.tensor_scalar_max(slot_ids[:, :, 2, :], sid[:].rearrange(pair, q=2), 0.0))
            then(v.scalar_tensor_tensor(sid[:], empty[:], float(P), tab[:, 0:NS], ALU.mult, ALU.add))
            then(v.tensor_scalar_add(sid[:], sid[:], -float(P)))
            then(v.scalar_tensor_tensor(empty[:], empty[:], 0.0, trash[:].rearrange("p s q -> p (s q)"),
                                        ALU.is_equal, ALU.mult))
            then(v.tensor_scalar(above[:], sid[:], float(N), -float(N), ALU.is_ge, ALU.mult))
            then(v.tensor_tensor(sid[:], sid[:], above[:], ALU.add))
            v.tensor_tensor(slot_ids[:, :, 1, :], sid[:].rearrange(pair, q=2), empty[:].rearrange(pair, q=2), ALU.add)\
                .then_inc(sem("ids_made"), 1)
            v.tensor_scalar_max(slot_ids[:, :, 0, :], sid[:].rearrange(pair, q=2), 0.0).then_inc(sem("ids_made"), 1)

            def rows_lo(gq, c):
                if within_st(gq, c):
                    dve.wait_ge(sem("xT_hi_made"), 10 * gq + c + 1)
                    v.tensor_tensor(xT_lo[:, c % 2].rearrange("p c t -> p (c t)"), banks[:, XT, :],
                                    xT_hi[:, c % 2].rearrange("p c t -> p (c t)").bitcast(f32), ALU.subtract)\
                        .then_inc(sem("xT_lo_made"), 1)

            dve.wait_ge(sem("ids_made"), 2)
            rows_lo(0, 0)
            dve.wait_ge(load_b2, 16)

            def expert_step(gq, c):
                if within_st(gq, c - 2):
                    st, u = 10 * gq + c - 2, c % 2
                    e = 2 * gq + (c - 2) // SPE
                    dve.wait_ge(sem("fc2_done"), st + 1)
                    wait(dve, scattered[u], 32 * (5 * gq + (c - 2) // 2))
                    v.tensor_tensor(y_sb[:, u], banks[:, YB + u, :].rearrange("p (q d) -> p q d", d=D),
                                    b2_sb[:, ds(e, 1), :].to_broadcast([P, 2, D]), ALU.add).then_inc(sem("y_made"), 1)
                rows_lo(gq, c + 1)
                if within_st(gq, c):
                    st, u = 10 * gq + c, c % 2
                    for n in range(HJ // 2):
                        raw = hraw[:, n]
                        hi, lo = h_hi[:, u, 2 * n:2 * n + 2, :], h_lo[:, u, 2 * n:2 * n + 2, :]
                        dve.wait_ge(sem("h_made"), HJ * st + 2 * n + 2)
                        if n == 0:
                            wait(dve, sem("fc2_done"), st - 1)
                        v.tensor_copy(hi, raw).then_inc(sem("h_hi_made"), 1)
                        dve.wait_ge(sem("h_hi_made"), 4 * st + n + 1)
                        v.tensor_tensor(lo, raw, hi.bitcast(f32), ALU.subtract).then_inc(sem("h_lo_made"), 1)

            expert_steps(dve, expert_step)

            dve.wait_ge(sem("beta_added"), NT)

            def combine(j, c):
                s = RING * j + c
                if within(s, NG):
                    dve.wait_ge(load_res[c], 16 * (j + 1))
                    for q in range(GT):
                        v.bn_stats(st_d[:, c, q, :], res[:, ds(s * GT + q, 1), :].rearrange("p a d -> p (a d)"))\
                            .then_inc(sem("st3_made"), 1)
                if within(s - 1, NG):
                    r = (c - 1) % RING
                    dve.wait_ge(sem("rstd3_made"), s)
                    v.scalar_tensor_tensor(nmr_d[:, r, :], mv_d[:, r, :, 0], -1.0, rstd_d[:, r, :],
                                           ALU.mult, ALU.mult).then_inc(sem("nmr_made"), 1)
                if within(s, NG):
                    dve.wait_ge(sem("st3_made"), GT * (s + 1))
                if within(s - 3, NG):
                    t = ds((s - 3) * GT, GT)
                    dve.wait_ge(sem("z_scaled"), GT * (s - 2))
                    v.tensor_tensor(z[:, t, :], z[:, t, :], X[:, t, :], ALU.add).then_inc(sem("out_made"), 1)
                if within(s, NG):
                    for q in range(GT):
                        v.bn_aggr(mv_d[:, c, q, :], st_d[:, c, q, :]).then_inc(sem("mv3_made"), 1)
                    dve.wait_ge(sem("mv3_made"), GT * (s + 1))
                    v.tensor_scalar_add(var_d[:, c, :], mv_d[:, c, :, 1], EPS_LN).then_inc(sem("var3_made"), 1)

            combine_steps(dve, combine)


_OUT_SHAPE = (4, 1024, 256)


def kernel(**inputs):
    import numpy as np
    import concourse.bacc as bacc
    from concourse import mybir as mb
    from concourse.bass_utils import run_bass_kernel_spmd

    def arr(name):
        return np.asarray(inputs[name])

    x, ctx = arr("x"), arr("ctx_1024")
    heads, dh = 16, 16
    w_kv = arr("L0_xattn_w_kv").reshape(heads, 2, dh, -1)
    b_kv = arr("L0_xattn_b_kv").reshape(heads, 2, dh)
    e, h, d = arr("L0_ffn_fc1_w").shape
    data = {
        "x": x.reshape(-1, x.shape[-1]),
        "ctxT": ctx.transpose(2, 0, 1),
        "wqT": arr("L0_xattn_w_q").T,
        "bq": arr("L0_xattn_b_q").reshape(-1, 128).T,
        "wkT": w_kv[:, 0].reshape(heads * dh, -1).T,
        "bk": b_kv[:, 0].reshape(-1, 128).T,
        "wvT": w_kv[:, 1].reshape(heads * dh, -1).T,
        "bv": b_kv[:, 1].reshape(-1),
        "woT": arr("L0_xattn_w_out").T,
        "bo": arr("L0_xattn_b_out"),
        "wg": arr("L0_ffn_wg"),
        "w1T": arr("L0_ffn_fc1_w").transpose(0, 2, 1),
        "b1T": arr("L0_ffn_fc1_b").reshape(e * h // 128, 128).T,
        "w2": arr("L0_ffn_fc2_w"),
        "b2": arr("L0_ffn_fc2_b"),
        "gamma": arr("L0_ffn_ln_gamma"),
        "beta": arr("L0_ffn_ln_beta"),
    }
    nc = bacc.Bacc("TRN2", target_bir_lowering=False, num_devices=1)
    arrays, args = {}, []
    for name, a in data.items():
        a = np.ascontiguousarray(a)
        arrays[f"in_{name}"] = a
        args.append(nc.dram_tensor(f"in_{name}", a.shape, mb.dt.from_np(a.dtype), kind="ExternalInput").ap())
    out = nc.dram_tensor("out", [x.shape[0] * x.shape[1], x.shape[2]], mb.dt.float32, kind="ExternalOutput").ap()
    xattn_moe_kernel(nc, *args, out)
    r = run_bass_kernel_spmd(nc, [arrays], core_ids=[0])
    return r.results[0]["out"].reshape(_OUT_SHAPE)
```

```python
import concourse.bass as bass
from concourse import mybir
from contextlib import ExitStack


def xattn_moe_kernel(nc, x, ctxT, wqT, bq, wkT, bk, wvT, bv, woT, bo, wg, w1T, b1T, w2, b2, gamma, beta, out):
    f32, f32r, bf16, i32 = mybir.dt.float32, mybir.dt.float32r, mybir.dt.bfloat16, mybir.dt.int32
    ALU, ACT, AX = mybir.AluOpType, mybir.ActivationFunctionType, mybir.AxisListType.X
    ds = bass.ds

    P = 128
    N, D = x.shape
    NT = N // P
    DC = D // P
    _, NB, NK = ctxT.shape
    TPB = NT // NB
    NH, DH = 16, 16
    HH = NH // 2
    KC = HH // 2 * NK
    KH = HH * NK
    NJ = 5
    JW = 124
    JS = JW - 1
    VW = P + HH
    assert JS * (NJ - 1) + JW == KH
    NE, _, HID = w1T.shape
    HJ = HID // P
    CAP = 2 * int(1.25 * ((N + NE - 1) // NE))
    NS = NE * CAP // P
    NST = NS // 2
    SPE = CAP // (2 * P)
    NR = 2
    NC = NR * NT
    EPS_LN, EPS_GATE = 1e-5, 1.1920929e-07
    SCALE = float(DH) ** -0.5
    PAIRS = NT // 2

    xn_rows = nc.dram_tensor("xn_rows", [N, D], f32, kind="Internal").ap()
    sum_rows = nc.dram_tensor("sum_rows", [N + 4 * P, D], f32, kind="Internal").ap()
    gate_rows = nc.dram_tensor("gate_rows", [P * NC, 1], f32, kind="Internal").ap()
    x_t = x.rearrange("(t p) d -> p t d", p=P)
    xn_t = xn_rows.rearrange("(t p) d -> p t d", p=P)
    out_t = out.rearrange("(t p) d -> p t d", p=P)
    sum_t = sum_rows[0:N, :].rearrange("(t p) d -> p t d", p=P)

    def wait(engine, sem, value):
        if not isinstance(value, int) or value > 0:
            engine.wait_ge(sem, value)

    def in_register(engine, value):
        return value if isinstance(value, int) else engine.snap(value)

    def within(t, n):
        return not isinstance(t, int) or 0 <= t < n

    def row(ap):
        return ap.rearrange("(a n) -> a n", a=1).to_broadcast([P, ap.shape[0]])

    sems = {}

    root, only_attn, only_moe = ExitStack(), ExitStack(), ExitStack()
    with root:
        def sb(name, shape, dt=f32, where=root):
            return where.enter_context(nc.sbuf_tensor(name, shape, dt))

        X = sb("X", [P, NT, D])
        w1raw = sb("w1raw", [P, DC, HID])
        w2raw = sb("w2raw", [P, HJ, D])
        ident = sb("ident", [P, P])
        logits = sb("logits", [P, NT, NE])
        gates = sb("gates", [P, NR, NT])
        tokens_e = sb("tokens_e", [P, NE], i32)
        slot_ids = sb("slot_ids", [P, NST, 3, 2], i32)
        b1_sb = sb("b1_sb", [P, NE * HJ])
        b1_now = sb("b1_now", [P, 2, HJ])
        silu_warm = sb("silu_warm", [P, 1])
        minus_half = sb("minus_half", [P, 4])
        upper = sb("upper", [P, P], bf16)
        gamma_sb, beta_sb = sb("gamma_sb", [P, D]), sb("beta_sb", [P, D])
        ones_bf = sb("ones_bf", [P, P], bf16)
        iota_lo = sb("iota_lo", [P, P], bf16)
        iota_hi = sb("iota_hi", [P, NS], bf16)
        my_row = sb("my_row", [P, 1])

        A = only_attn
        KH_hi = sb("KH_hi", [P, NB * 2 * KH], f32r, A)
        KH_lo = sb("KH_lo", [P, NB * 2 * KH], f32r, A)
        VB = sb("VB", [JW, NB * 2 * NJ * VW], f32, A)
        probs = sb("probs", [P, 2, 2 * KH], f32, A)
        probsT = sb("probsT", [JW, 2 * NJ, P], f32, A)
        wq_hi, wq_lo, wo_hi, wo_lo = (sb(n, [P, DC, D], f32r, A) for n in ("wq_hi", "wq_lo", "wo_hi", "wo_lo"))
        wg_sb = sb("wg_sb", [P, DC, P], f32, A)
        bq_sb, bk_sb = sb("bq_sb", [P, DC], f32, A), sb("bk_sb", [P, DC], f32, A)
        bv_sb, bo_sb = sb("bv_sb", [P, D], f32, A), sb("bo_sb", [P, D], f32, A)
        head_of_feature = sb("head_of_feature", [P, HH], f32, A)
        head_of_row = sb("head_of_row", [JW, NJ, HH], f32, A)
        xn1 = sb("xn1", [P, 2, D], f32, A)
        xn1T_hi, xn1T_lo = sb("xn1T_hi", [P, DC, 2 * P], f32r, A), sb("xn1T_lo", [P, DC, 2 * P], f32r, A)
        q_hi, q_lo = sb("q_hi", [P, DC, 2 * P], f32r, A), sb("q_lo", [P, DC, 2 * P], f32r, A)
        rowmax = sb("rowmax", [P, 2, HH], f32, A)
        rden = sb("rden", [P, 2, HH], f32, A)
        vals = sb("vals", [P, D], f32, A)
        valsT_hi, valsT_lo = sb("valsT_hi", [P, DC, P], f32r, A), sb("valsT_lo", [P, DC, P], f32r, A)
        xn2 = sb("xn2", [P, 2, D], f32, A)
        xn2T = sb("xn2T", [P, DC, P], f32, A)
        zero_row = sb("zero_row", [P, D], f32, A)
        st1, mv1 = sb("st1", [P, 2, 6], f32, A), sb("mv1", [P, 2, 2], f32, A)
        var1, rstd1 = sb("var1", [P, 2], f32, A), sb("rstd1", [P, 2], f32, A)
        st2, mv2 = sb("st2", [P, 2, 6], f32, A), sb("mv2", [P, 2, 2], f32, A)
        var2, rstd2 = sb("var2", [P, 2], f32, A), sb("rstd2", [P, 2], f32, A)
        first_of = sb("first_of", [P, NE], f32, A)
        keep_going = sb("keep_going", [P, NE, NC], f32, A)
        col_no = sb("col_no", [P, NC], f32, A)
        trash = sb("trash", [P, NS // 4, 4], f32, A)
        S = ExitStack()
        ctx_sb = sb("ctx_sb", [P, DC, NB * NK], f32, S)
        kT = sb("kT", [P, DC, NB * NK], f32, S)
        kT_hi, kT_lo = sb("kT_hi", [P, DC, NB * NK], f32r, S), sb("kT_lo", [P, DC, NB * NK], f32, S)
        v_sb = sb("v_sb", [NK, NB, D], f32, S)
        v_hi, v_lo = sb("v_hi", [NK, NB, D], f32r, S), sb("v_lo", [NK, NB, D], f32r, S)
        key_of_row_r = sb("key_of_row_r", [NK, HH, NK], f32r, S)
        key_of_row = sb("key_of_row", [NK, HH, NK], f32, S)
        wq_sb, wk_sb, wv_sb, wo_sb = (sb(n, [P, DC, D], f32, S) for n in ("wq_sb", "wk_sb", "wv_sb", "wo_sb"))
        S.close()
        score = sb("score", [P, NT, NE], f32, A)
        score2 = sb("score2", [P, NT, NE], f32, A)
        weigh = sb("weigh", [P, NT, NE], f32, A)
        sel = sb("sel", [P, NR, NT, NE], bf16, A)
        tmax = sb("tmax", [P, NR, NT], f32, A)
        tpick = sb("tpick", [P, NR, NT], f32, A)
        tsum = sb("tsum", [P, NT], f32, A)
        trec = sb("trec", [P, NT], f32, A)
        scan_e = sb("scan_e", [P, NE, NC], f32, A)
        place = sb("place", [P, NR, NT, NE], f32, A)
        loc = sb("loc", [P, NC], f32, A)
        kept = sb("kept", [P, NC], f32, A)
        pos = sb("pos", [P, NC], f32, A)
        hi_i = sb("hi_i", [P, NC], i32, A)
        slot_hi = sb("slot_hi", [P, NC], f32, A)
        slot_lo = sb("slot_lo", [P, NC], f32, A)
        CH = 8
        oh_lo = sb("oh_lo", [P, 2, CH, P], bf16, A)
        oh_hi = sb("oh_hi", [P, 2, CH, NS], bf16, A)
        oh_id = sb("oh_id", [P, 2, CH, 2, NS], bf16, A)
        sid = sb("sid", [P, NS], f32, A)
        empty = sb("empty", [P, NS], f32, A)
        above = sb("above", [P, NS], f32, A)
        attn_top = nc.sbuf_bytes_remaining
        A.close()

        M = only_moe
        w1_hi, w1_lo = sb("w1_hi", [P, 2, DC, HID], f32r, M), sb("w1_lo", [P, 2, DC, HID], f32r, M)
        w2_hi, w2_lo = sb("w2_hi", [P, 2, HJ, D], f32r, M), sb("w2_lo", [P, 2, HJ, D], f32r, M)
        b2_sb = sb("b2_sb", [P, NE, D], f32, M)
        xg = sb("xg", [P, SPE, 2, D], f32, M)
        xT_hi, xT_lo = sb("xT_hi", [P, 2, DC, 2 * P], f32r, M), sb("xT_lo", [P, 2, DC, 2 * P], f32r, M)
        hraw = sb("hraw", [P, 4, 2, 2 * P], f32, M)
        h_hi, h_lo = sb("h_hi", [P, 2, HJ, 2 * P], f32r, M), sb("h_lo", [P, 2, HJ, 2 * P], f32r, M)
        y_sb = sb("y_sb", [P, 2, 2, D], f32, M)
        gate_s = sb("gate_s", [P, 2 * SPE, 2], f32, M)
        M.close()
        C = ExitStack()
        GT = 2
        NG = NT // GT
        RING = 4
        res = sb("res", [P, NT, D], f32, C)
        z = sb("z", [P, NT, D], f32, C)
        st_d, mv_d = sb("st_d", [P, RING, GT, 6], f32, C), sb("mv_d", [P, RING, GT, 2], f32, C)
        var_d, rstd_d, nmr_d = (sb(n, [P, RING, GT], f32, C) for n in ("var_d", "rstd_d", "nmr_d"))
        C.close()

        banks = root.enter_context(nc.psum_tensor("banks", [P, 8, 512], f32))
        PT, PV, TR, PJ = 4, 5, 6, 7
        QB, LB = 0, 1
        XT, YB = 4, 5

        for name in (
            "load_small load_wq load_wkv load_wo load_ctx load_wg load_b1 load_b2 load_gb load_w1 load_w2 trash_zeroed gates_stored "
            "cleared half_made ident_made masks_made wg_cleared zero_made v_ones_made k_lo_made route_consts "
            "rstd1_made x_biased rstd2_made xn1_centred xn2_centred xn2_made column_made b1_copied w_lo_made beta_added rstd3_made z_scaled "
            "key_rows_made kT_made w_hi_ready v_hi_made xn1T_hi_made q_hi_made pT_made probs_made valsT_hi_made xn2T_made logits_made router_exp row_made "
            "xT_hi_made h_made y_scaled w_hi_made z_made "
            "kT_done v_done v_rows_done xn1T_done q_done scores_done pT_done pv_done valsT_done out_done "
            "xn2T_done logits_done counted placed rows_transposed fc1_done fc2_done "
            "kT_split v_made v_lo_made v_placed k_hi_made wq_split wo_split st1_made mv1_made var1_made xn1_made "
            "xn1T_lo_made q_lo_made max_made shifted rden_made vals_made valsT_lo_made x2_made st2_made mv2_made "
            "var2_made router_shifted sel_made routed tokens_counted gates_made onehot_made ids_made xT_lo_made "
            "h_hi_made h_lo_made y_made st3_made mv3_made var3_made nmr_made out_made"
        ).split():
            sems[name] = root.enter_context(nc.semaphore(name))

        def sem(name):
            return sems[name]

        def dma_sem(name):
            return root.enter_context(nc.semaphore(name))

        load_x = [dma_sem(f"load_x{i}") for i in range(4)]
        load_small, load_wq, load_wkv, load_wo = sem("load_small"), sem("load_wq"), sem("load_wkv"), sem("load_wo")
        load_ctx, load_wg, load_b1, load_b2 = sem("load_ctx"), sem("load_wg"), sem("load_b1"), sem("load_b2")
        load_gb, load_w1, load_w2 = sem("load_gb"), sem("load_w1"), sem("load_w2")
        xn_stored = [dma_sem(f"xn_stored{u}") for u in range(2)]
        gathered = [dma_sem(f"gathered{u}") for u in range(SPE)]
        scattered = [dma_sem(f"scattered{u}") for u in range(2)]
        load_gate = [dma_sem(f"load_gate{u}") for u in range(2)]
        load_res = [dma_sem(f"load_res{u}") for u in range(RING)]
        stored = dma_sem("stored")

        block = root.enter_context(nc.Block())

        def attention_steps(engine, step, spread=None):
            for i in (0, 1, 2):
                for u in (0, 1):
                    step(i, u)
                    if spread is not None and 2 * i + u < NB - 1:
                        spread(2 * i + u + 1)
            with engine.Fori(3, PAIRS - 2) as i:
                step(i, 0)
                step(i, 1)
            for i in (PAIRS - 2, PAIRS - 1, PAIRS):
                step(i, 0)
                step(i, 1)
            step(PAIRS + 1, 0)

        def expert_steps(engine, step):
            for c in range(SPE):
                step(0, c)
            with engine.Fori(0, 3) as g:
                for c in range(SPE, 3 * SPE):
                    step(g, c)
            for c in range(7 * SPE, NST + 3):
                step(0, c)

        def combine_steps(engine, step):
            for c in range(RING):
                step(0, c)
            with engine.Fori(1, NG // RING) as j:
                for c in range(RING):
                    step(j, c)
            for c in range(4):
                step(NG // RING, c)

        def batch_of(t):
            if isinstance(t, int):
                return t // TPB
            return nc.s_assert_within(t >> 3, 0, NB - 1,
                                      skip_runtime_bounds_check_because="t is a token tile of the loop, below 32")

        ST_ROWS = 2 * P
        FEW_FROM = 3
        EARLY, LATE = slice(0, NT - 4), slice(NT - 4, NT)

        V_BANKS = [(PT, PV, TR, PJ)] * 2 + [(TR, PJ)] * 2

        def within_st(g, c):
            return not isinstance(g, int) or 0 <= 10 * g + c < NST

        def w_parts(par, n):
            if n < 2:
                return w1_hi[:, par, n, :], w1_lo[:, par, n, :], w1raw[:, n, :]
            j = slice(4 * (n - 2), 4 * (n - 1))
            return w2_hi[:, par, j, :], w2_lo[:, par, j, :], w2raw[:, j, :]

        @block.sync
        def _(sp):
            sp.dma_start(ctx_sb[:], ctxT.rearrange("(c p) b k -> p c (b k)", p=P)).then_inc(load_ctx, 16)
            sp.dma_start(wk_sb[:], wkT.rearrange("(c p) o -> p c o", p=P)).then_inc(load_wkv, 16)
            sp.dma_start(X[:, 0:4, :], x_t[:, 0:4, :]).then_inc(load_x[0], 16)
            sp.dma_start(wv_sb[:], wvT.rearrange("(c p) o -> p c o", p=P)).then_inc(load_wkv, 16)
            sp.dma_start(wq_sb[:], wqT.rearrange("(c p) o -> p c o", p=P)).then_inc(load_wq, 16)
            for n, (a, b) in enumerate(((4, 12), (12, 22), (22, NT))):
                sp.dma_start(X[:, a:b, :], x_t[:, a:b, :]).then_inc(load_x[n + 1], 16)
            sp.dma_start(wo_sb[:], woT.rearrange("(c p) o -> p c o", p=P)).then_inc(load_wo, 16)
            sp.dma_start(w1raw[:], w1T[0].rearrange("(c p) h -> p c h", p=P)).then_inc(load_w1, 16)
            sp.dma_start(w2raw[:], w2[0].rearrange("(j p) d -> p j d", p=P)).then_inc(load_w2, 16)
            sp.wait_ge(sem("zero_made"), 1)
            sp.dma_start(sum_rows[N:N + 4 * P, :].rearrange("(q p) d -> p q d", p=P),
                         zero_row[:].unsqueeze(1).to_broadcast([P, 4, D])).then_inc(sem("trash_zeroed"), 16)
            sp.dma_start(gamma_sb[:], row(gamma)).then_inc(load_gb, 16)
            sp.dma_start(beta_sb[:], row(beta)).then_inc(load_gb, 16)

            def store_xn(i, u):
                if within(2 * i + u - 3, NT):
                    sp.wait_ge(sem("xn2_made"), 2 * i + u - 2)
                    for rows in (xn_t, sum_t):
                        sp.dma_start(rows[:, ds(2 * i + u - 3, 1), :].rearrange("p a d -> p (a d)"),
                                     xn2[:, 1 - u, :]).then_inc(xn_stored[1 - u], 16)

            attention_steps(sp, store_xn)
            sp.wait_ge(sem("logits_made"), NT)
            sp.dma_start(b2_sb[:], b2.rearrange("(a e) d -> a e d", a=1).to_broadcast([P, NE, D])).then_inc(load_b2, 16)
            with sp.Fori(1, NE) as e:
                sp.wait_ge(sem("w_hi_made"), 4 * e - 2)
                sp.wait_ge(sem("w_lo_made"), 4 * e - 2)
                sp.dma_start(w1raw[:], w1T[ds(e, 1)].rearrange("a (c p) h -> p (a c) h", p=P)).then_inc(load_w1, 16)
                sp.wait_ge(sem("w_hi_made"), 4 * e)
                sp.wait_ge(sem("w_lo_made"), 4 * e)
                sp.dma_start(w2raw[:], w2[ds(e, 1)].rearrange("a (j p) d -> p (a j) d", p=P)).then_inc(load_w2, 16)
            sp.wait_ge(scattered[0], 32 * (NST // 2))
            sp.wait_ge(scattered[1], 32 * (NST // 2))

            for g in range(NG + 8):
                if within(g, NG):
                    c, t = g % RING, slice(g * GT, (g + 1) * GT)
                    wait(sp, load_res[c], 16 * (g // RING))
                    sp.dma_start(res[:, t, :], sum_t[:, t, :]).then_inc(load_res[c], 16)
                if within(g - 8, NG):
                    t = slice((g - 8) * GT, (g - 7) * GT)
                    sp.wait_ge(sem("out_made"), g - 7)
                    sp.dma_start(out_t[:, t, :], z[:, t, :]).then_inc(stored, 16)
            sp.wait_ge(stored, 16 * NG)

        @block.gpsimd
        def _(pool):
            g = nc.gpsimd
            g.memset(ident[:], 0.0).then_inc(sem("cleared"), 1)
            g.memset(key_of_row[:], 0.0).then_inc(sem("cleared"), 1)
            g.memset(head_of_feature[:], 1.0).then_inc(sem("cleared"), 1)
            g.memset(head_of_row[:], 1.0).then_inc(sem("cleared"), 1)
            g.memset(minus_half[:], -0.5).then_inc(sem("half_made"), 1)
            pool.wait_ge(sem("cleared"), 4)
            g.affine_select(out=ident[:], in_=ident[:], compare_op=ALU.not_equal, fill=1.0, base=0,
                            pattern=[[-1, P]], channel_multiplier=1).then_inc(sem("ident_made"), 1)
            g.affine_select(out=key_of_row[:], in_=key_of_row[:], compare_op=ALU.not_equal, fill=1.0, base=0,
                            pattern=[[0, HH], [-1, NK]], channel_multiplier=1).then_inc(sem("masks_made"), 1)
            g.affine_select(out=head_of_feature[:], in_=head_of_feature[:], compare_op=ALU.is_ge, fill=0.0, base=0,
                            pattern=[[-DH, HH]], channel_multiplier=1).then_inc(sem("cleared"), 1)
            g.affine_select(out=head_of_row[:], in_=head_of_row[:], compare_op=ALU.is_ge, fill=0.0, base=0,
                            pattern=[[JS, NJ], [-NK, HH]], channel_multiplier=1).then_inc(sem("cleared"), 1)
            pool.wait_ge(sem("cleared"), 6)
            g.affine_select(out=head_of_feature[:], in_=head_of_feature[:], compare_op=ALU.is_ge, fill=0.0,
                            base=DH - 1, pattern=[[DH, HH]], channel_multiplier=-1).then_inc(sem("masks_made"), 1)
            g.affine_select(out=head_of_row[:], in_=head_of_row[:], compare_op=ALU.is_ge, fill=0.0,
                            base=NK - 1, pattern=[[-JS, NJ], [NK, HH]], channel_multiplier=-1).then_inc(sem("cleared"), 1)
            pool.wait_ge(sem("cleared"), 7)
            g.memset(head_of_row[0:1, 1:NJ, :], 0.0).then_inc(sem("masks_made"), 1)
            g.memset(wg_sb[:], 0.0).then_inc(sem("wg_cleared"), 1)
            g.memset(zero_row[:], 0.0).then_inc(sem("zero_made"), 1)
            pool.wait_ge(sem("masks_made"), 3)
            vb = VB[:].rearrange("r (b f j w) -> r (b f) j w", f=2, j=NJ, w=VW)
            for bf in range(2 * NB):
                g.tensor_copy(vb[:, bf, :, P:VW], head_of_row[:]).then_inc(sem("v_ones_made"), 1)

            def rstd_first(j):
                if within(j, PAIRS):
                    pool.wait_ge(sem("var1_made"), j + 1)
                    g.tensor_tensor(rstd1[:], var1[:], minus_half[:, 0:2], ALU.pow).then_inc(sem("rstd1_made"), 1)

            def spread_lo(b):
                for f in range(DC):
                    g.tensor_tensor(KH_lo[:, (b * 2 + f) * KH:(b * 2 + f + 1) * KH].rearrange("p (h k) -> p h k", k=NK),
                                    kT_lo[:, f, b * NK:(b + 1) * NK].unsqueeze(1).to_broadcast([P, HH, NK]),
                                    head_of_feature[:].unsqueeze(2).to_broadcast([P, HH, NK]),
                                    ALU.mult).then_inc(sem("k_lo_made"), 1)

            rstd_first(0)
            pool.wait_ge(sem("kT_split"), 2 * DC)
            spread_lo(0)
            rstd_first(1)
            for b in range(1, NB):
                spread_lo(b)
            g.memset(ones_bf[:], 1.0).then_inc(sem("route_consts"), 1)
            g.memset(upper[:], 0.0).then_inc(sem("cleared"), 1)
            g.memset(keep_going[:], 1.0).then_inc(sem("cleared"), 1)
            pool.wait_ge(sem("cleared"), 9)
            g.affine_select(out=upper[:], in_=upper[:], compare_op=ALU.is_ge, fill=-1.0, base=0,
                            pattern=[[1, P]], channel_multiplier=-1).then_inc(sem("route_consts"), 1)
            g.memset(keep_going[:, :, 0:1], 0.0).then_inc(sem("route_consts"), 1)
            g.iota(iota_lo[:], pattern=[[1, P]], base=0, channel_multiplier=0,
                   allow_small_or_imprecise_dtypes=True).then_inc(sem("route_consts"), 1)
            g.iota(iota_hi[:], pattern=[[1, NS]], base=1, channel_multiplier=0,
                   allow_small_or_imprecise_dtypes=True).then_inc(sem("route_consts"), 1)
            g.iota(my_row[:], pattern=[[1, 1]], base=0, channel_multiplier=1,
                   allow_small_or_imprecise_dtypes=True).then_inc(sem("route_consts"), 1)
            g.iota(trash[:], pattern=[[0, NS // 4], [P, 4]], base=N + P, channel_multiplier=1,
                   allow_small_or_imprecise_dtypes=True).then_inc(sem("route_consts"), 1)
            g.iota(col_no[:], pattern=[[1, NC]], base=1, channel_multiplier=0,
                   allow_small_or_imprecise_dtypes=True).then_inc(sem("route_consts"), 1)
            g.iota(first_of[:], pattern=[[-1, NE]], base=NE, channel_multiplier=0,
                   allow_small_or_imprecise_dtypes=True).then_inc(sem("route_consts"), 1)

            def bias(j):
                if within(j, PAIRS):
                    pool.wait_ge(sem("xn1_made"), 2 * j + 2)
                    for v in range(2):
                        xt = X[:, ds(2 * j + v, 1), :].rearrange("p a d -> p (a d)")
                        g.tensor_tensor(xt, xt, bo_sb[:], ALU.add).then_inc(sem("x_biased"), 1)

            pool.wait_ge(load_small, 16 * 4)
            bias(0)

            def centre(out, tile, mean, name):
                rows = X[:, ds(tile, 1), :].rearrange("p a d -> p (a d)")
                g.tensor_tensor(out, rows, mean.to_broadcast([P, D]), ALU.subtract).then_inc(sem(name), 1)

            def scale(out, rstd, name):
                g.tensor_tensor(out, out, rstd.to_broadcast([P, D]), ALU.mult).then_inc(sem(name), 1)

            def step(i, u):
                t = 2 * i + u
                if u == 1 and within(i + 2, PAIRS):
                    for w in range(2):
                        if w == 0:
                            pool.wait_ge(sem("xn1T_done"), i + 2)
                            pool.wait_ge(sem("rstd1_made"), i + 3)
                        centre(xn1[:, w, :], t + 3 + w, mv1[:, w, 0:1], "xn1_centred")
                    pool.wait_ge(sem("xn1_centred"), 2 * (i + 1))
                    for w in range(2):
                        scale(xn1[:, w, :], rstd1[:, w:w + 1], "xn1_made")
                if within(t - 2, NT):
                    pool.wait_ge(sem("var2_made"), t - 1)
                    g.tensor_tensor(rstd2[:, u:u + 1], var2[:, u:u + 1], minus_half[:, 0:1], ALU.pow)\
                        .then_inc(sem("rstd2_made"), 1)
                    wait(pool, sem("xn2T_done"), t - 3)
                    wait(pool, xn_stored[u], 32 * (i - 1))
                    centre(xn2[:, u, :], t - 2, mv2[:, u, 0:1], "xn2_centred")
                    pool.wait_ge(sem("rstd2_made"), t - 1)
                    pool.wait_ge(sem("xn2_centred"), t - 1)
                    scale(xn2[:, u, :], rstd2[:, u:u + 1], "xn2_made")
                if u == 0:
                    bias(i + 1)
                    rstd_first(i + 2)

            attention_steps(pool, step)

            AHEAD = SPE - 1

            def gather(st):
                if within(st, NST):
                    u = st % SPE
                    wait(pool, sem("rows_transposed"), st - SPE + 1)
                    for q in range(2):
                        g.indirect_dma_start(xg[:, u, q, :], None, xn_rows,
                                             bass.IndirectOffsetOnAxis(ap=slot_ids[:, st, 0, q:q + 1], axis=0),
                                             bounds_check=N - 1, oob_is_err=False).then_inc(gathered[u], 16)

            def gather_gates(st):
                if within(st, NST):
                    u, k = st % 2, st % (2 * SPE)
                    wait(pool, load_gate[u], 32 * (st // 2))
                    wait(pool, sem("y_scaled"), st + 1 - 2 * SPE)
                    for q in range(2):
                        g.indirect_dma_start(gate_s[:, k, q:q + 1], None, gate_rows,
                                             bass.IndirectOffsetOnAxis(ap=slot_ids[:, st, 2, q:q + 1], axis=0),
                                             bounds_check=P * NC - 1, oob_is_err=False).then_inc(load_gate[u], 16)

            def scatter(st):
                if within(st, NST):
                    u = st % 2
                    wait(pool, scattered[1 - u], 32 * ((st + 1) // 2))
                    pool.wait_ge(sem("y_scaled"), st + 1)
                    for q in range(2):
                        g.indirect_dma_start(sum_rows, bass.IndirectOffsetOnAxis(ap=slot_ids[:, st, 1, q:q + 1], axis=0),
                                             y_sb[:, u, q, :], None, bounds_check=N + 4 * P - 1, oob_is_err=False,
                                             compute_op=ALU.add).then_inc(scattered[u], 16)

            def split_first_quarter(n):
                pool.wait_ge(load_w1 if n < 2 else load_w2, 16)
                pool.wait_ge(sem("w_hi_made"), n + 1)
                if n == 0:
                    g.tensor_copy(b1_now[:, 0, :], b1_sb[:, 0:HJ]).then_inc(sem("b1_copied"), 1)
                hi, lo, raw = w_parts(0, n)
                g.tensor_tensor(lo, raw, hi.bitcast(f32), ALU.subtract).then_inc(sem("w_lo_made"), 1)

            pool.wait_ge(load_b1, 16)
            pool.wait_ge(sem("logits_made"), NT)
            for n in range(4):
                split_first_quarter(n)
            for k in range(NC // CH):
                pool.wait_ge(sem("onehot_made"), 2 * k + 1)
                wait(pool, sem("placed"), CH * (k - 1))
                g.tensor_tensor(oh_id[:, k % 2, :, 1, :], oh_hi[:, k % 2],
                                col_no[:, k * CH:(k + 1) * CH].unsqueeze(2).to_broadcast([P, CH, NS]), ALU.mult)\
                    .then_inc(sem("column_made"), 1)
            pool.wait_ge(sem("ids_made"), 1)
            for u in range(2):
                pool.wait_ge(xn_stored[u], 32 * PAIRS)
            gather(0)
            gather(1)
            pool.wait_ge(load_gb, 32)
            pool.wait_ge(sem("trash_zeroed"), 16)
            pool.wait_ge(sem("gates_stored"), 16)
            pool.wait_ge(sem("ids_made"), 3)
            gather_gates(0)
            for st in range(2, AHEAD):
                gather(st)

            for st in range(NST + 2):
                gather(st + AHEAD)
                gather_gates(st + 1)
                scatter(st - 2)
                if st < NT:
                    g.tensor_tensor(X[:, st, :], X[:, st, :], beta_sb[:], ALU.add).then_inc(sem("beta_added"), 1)

            def combine(j, c):
                s = RING * j + c
                if within(s, NG):
                    pool.wait_ge(sem("var3_made"), s + 1)
                    g.tensor_tensor(rstd_d[:, c, :], var_d[:, c, :], minus_half[:, 0:GT], ALU.pow)\
                        .then_inc(sem("rstd3_made"), 1)
                if within(s - 2, NG):
                    for q in range(GT):
                        pool.wait_ge(sem("z_made"), GT * (s - 2) + q + 1)
                        zt = z[:, ds((s - 2) * GT + q, 1), :].rearrange("p a d -> p (a d)")
                        g.tensor_tensor(zt, zt, gamma_sb[:], ALU.mult).then_inc(sem("z_scaled"), 1)

            combine_steps(pool, combine)

        @block.scalar
        def _(act):
            a = nc.scalar
            act.dma_start(bq_sb[:], bq).then_inc(load_small, 16)
            act.dma_start(bk_sb[:], bk).then_inc(load_small, 16)
            act.dma_start(bv_sb[:], row(bv)).then_inc(load_small, 16)
            act.dma_start(bo_sb[:], row(bo)).then_inc(load_small, 16)
            act.dma_start(b1_sb[:], b1T).then_inc(load_b1, 16)
            act.wait_ge(sem("wg_cleared"), 1)
            act.dma_start(wg_sb[:, :, 0:NE], wg.rearrange("(c p) e -> p c e", p=P)).then_inc(load_wg, 16)
            act.wait_ge(load_small, 16 * 4)
            for f in range(DC):
                act.wait_ge(sem("kT_done"), f + 1)
                a.activation(kT[:, f, :], banks[:, f, 0:NB * NK], ACT.Identity, bias=bk_sb[:, f:f + 1])\
                    .then_inc(sem("kT_made"), 1)

            act.wait_ge(sem("masks_made"), 3)
            a.activation(key_of_row_r[:], key_of_row[:], ACT.Copy).then_inc(sem("key_rows_made"), 1)
            act.wait_ge(load_wq, 16)
            a.activation(wq_hi[:], wq_sb[:], ACT.Copy).then_inc(sem("w_hi_ready"), 1)

            def first_layernorm(j):
                if within(j, PAIRS):
                    act.wait_ge(sem("xn1T_done"), j + 1)
                    a.activation(xn1T_hi[:].rearrange("p c t -> p (c t)"), banks[:, LB, :], ACT.Copy)\
                        .then_inc(sem("xn1T_hi_made"), 1)

            def queries(j):
                if within(j, PAIRS):
                    act.wait_ge(sem("q_done"), j + 1)
                    for f in range(DC):
                        a.activation(q_hi[:, f, :], banks[:, QB, f * 256:(f + 1) * 256], ACT.Identity,
                                     bias=bq_sb[:, f:f + 1]).then_inc(sem("q_hi_made"), 1)

            first_layernorm(0)
            act.wait_ge(sem("v_made"), NB)
            a.activation(v_hi[:], v_sb[:], ACT.Copy).then_inc(sem("v_hi_made"), 1)
            queries(0)
            act.wait_ge(load_wo, 16)
            a.activation(wo_hi[:], wo_sb[:], ACT.Copy).then_inc(sem("w_hi_ready"), 1)

            def router_exp(part, tiles):
                act.wait_ge(sem("router_shifted"), part + 1)
                a.activation(score[:, tiles, :], score[:, tiles, :], ACT.Exp).then_inc(sem("router_exp"), 1)

            def step(i, u):
                t = 2 * i + u
                if isinstance(i, int) and i == PAIRS + 1:
                    router_exp(0, EARLY)

                def probs_transposed(n):
                    if within(t - 1, NT):
                        f, w = n // 2, (3, 2)[n % 2]
                        j0 = NJ * f + 3 * (n % 2)
                        act.wait_ge(sem("pT_done"), 4 * (t - 1) + n + 1)
                        a.activation(probsT[:, j0:j0 + w, :].rearrange("r j q -> r (j q)"),
                                     banks[0:JW, PT, 0:w * P], ACT.Copy).then_inc(sem("pT_made"), 1)

                def exp(f):
                    if within(t, NT):
                        act.wait_ge(sem("shifted"), 2 * t + f + 1)
                        e = probs[:, u, f * KH:(f + 1) * KH]
                        a.activation(e, e, ACT.Exp, scale=SCALE).then_inc(sem("probs_made"), 1)

                probs_transposed(0)
                if within(t - 2, NT):
                    act.wait_ge(sem("valsT_done"), t - 1)
                    a.activation(valsT_hi[:].rearrange("p c q -> p (c q)"), banks[:, TR, 0:256], ACT.Copy)\
                        .then_inc(sem("valsT_hi_made"), 1)
                probs_transposed(1)
                exp(0)
                if u == 0:
                    first_layernorm(i + 1)
                else:
                    queries(i + 1)
                probs_transposed(2)
                probs_transposed(3)
                if within(t - 3, NT):
                    act.wait_ge(sem("xn2T_done"), t - 2)
                    a.activation(xn2T[:].rearrange("p c q -> p (c q)"), banks[:, TR, 256:512], ACT.Copy)\
                        .then_inc(sem("xn2T_made"), 1)
                exp(1)
                if within(t - 3, NT):
                    done = in_register(act, t - 2)
                    act.wait_ge(load_wg, 16)
                    act.wait_ge(sem("logits_done"), done)
                    a.activation(logits[:, ds(t - 3, 1), :].rearrange("p a e -> p (a e)"), banks[:, PJ, 256:256 + NE],
                                 ACT.Copy).then_inc(sem("logits_made"), 1)

            attention_steps(act, step)

            router_exp(1, LATE)

            def rows_of_chunk(k):
                act.wait_ge(sem("onehot_made"), 2 * k + 1)
                wait(act, sem("placed"), CH * (k - 1))
                a.activation(oh_id[:, k % 2, :, 0, :], oh_hi[:, k % 2], ACT.Copy, scale=my_row[:, 0:1])\
                    .then_inc(sem("row_made"), 1)

            def split_quarter(e, par, n):
                wait(act, sem("fc2_done"), SPE * (e - 1))
                wait(act, load_w1 if n < 2 else load_w2, 16 * (e + 1))
                hi, lo, raw = w_parts(par, n)
                a.activation(hi, raw, ACT.Copy).then_inc(sem("w_hi_made"), 1)

            def rows_hi(gq, c):
                if within_st(gq, c):
                    act.wait_ge(sem("rows_transposed"), 10 * gq + c + 1)
                    a.activation(xT_hi[:, c % 2].rearrange("p c t -> p (c t)"), banks[:, XT, :], ACT.Copy)\
                        .then_inc(sem("xT_hi_made"), 1)

            for n in range(4):
                split_quarter(0, 0, n)
            for k in range(NC // CH):
                rows_of_chunk(k)
            a.activation(silu_warm[:], my_row[:], ACT.Silu)
            act.wait_ge(sem("gates_made"), 1)
            act.dma_start(gate_rows.rearrange("(p c) a -> p (c a)", p=P), gates[:].rearrange("p r t -> p (r t)"))\
                .then_inc(sem("gates_stored"), 16)
            act.wait_ge(sem("ids_made"), 3)
            rows_hi(0, 0)

            def scale_results(gq, c):
                if within_st(gq, c):
                    act.wait_ge(load_gate[c % 2], 32 * (5 * gq + c // 2 + 1))
                    act.wait_ge(sem("y_made"), 10 * gq + c + 1)
                    for q in range(2):
                        y = y_sb[:, c % 2, q, :]
                        m = a.activation(y, y, ACT.Copy, scale=gate_s[:, c % (2 * SPE), q:q + 1])
                    m.then_inc(sem("y_scaled"), 1)

            def expert_step(gq, c):
                rows_hi(gq, c + 1)
                if within_st(gq, c):
                    st = 10 * gq + c
                    for j in range(HJ):
                        if j % 2 == 0:
                            wait(act, sem("h_lo_made"), 4 * (st - 1) + j // 2 + 1)
                            act.wait_ge(sem("fc1_done"), 4 * st + j // 2 + 1)
                        a.activation(hraw[:, j // 2, j % 2, :], banks[:, j // 2, (j % 2) * 256:(j % 2 + 1) * 256],
                                     ACT.Silu, bias=b1_now[:, (c // SPE) % 2, j:j + 1])\
                            .then_inc(sem("h_made"), 1)
                scale_results(gq, c - 2)
                e, s = 2 * gq + c // SPE + 1, c % SPE
                if s and within(e, NE):
                    split_quarter(e, (c // SPE + 1) % 2, s - 1)

            expert_steps(act, expert_step)

            def combine(j, c):
                s = RING * j + c
                if within(s - 1, NG):
                    act.wait_ge(sem("nmr_made"), s)
                    for q in range(GT):
                        t, r = ds((s - 1) * GT + q, 1), (c - 1) % RING
                        a.activation(z[:, t, :].rearrange("p a d -> p (a d)"), res[:, t, :].rearrange("p a d -> p (a d)"),
                                     ACT.Identity, scale=rstd_d[:, r, q:q + 1], bias=nmr_d[:, r, q:q + 1])\
                            .then_inc(sem("z_made"), 1)

            combine_steps(act, combine)

        @block.tensor
        def _(pe):
            t_ = nc.tensor

            def mm3(o, a_hi, a_lo, b_hi, b_lo, first, last):
                t_.matmul(o, a_hi, b_hi, start=first, stop=False)
                t_.matmul(o, a_hi, b_lo, start=False, stop=False)
                return t_.matmul(o, a_lo, b_hi, start=False, stop=last)

            pe.wait_ge(load_ctx, 16)
            pe.wait_ge(load_wkv, 32)
            for f in range(DC):
                for c in range(DC):
                    m = t_.matmul(banks[:, f, 0:NB * NK], wk_sb[:, c, f * P:(f + 1) * P], ctx_sb[:, c, :],
                                  start=(c == 0), stop=(c == DC - 1))
                m.then_inc(sem("kT_done"), 1)
            for b in range(NB):
                for c in range(DC):
                    m = t_.matmul(banks[0:NK, 2 + b // 2, (b % 2) * D:(b % 2 + 1) * D],
                                  ctx_sb[:, c, b * NK:(b + 1) * NK], wv_sb[:, c, :], start=(c == 0), stop=(c == DC - 1))
                m.then_inc(sem("v_done"), 1)
            def spread(b, banks_of):
                pe.wait_ge(sem("key_rows_made"), 1)
                pe.wait_ge(sem("v_lo_made"), 1)
                rows = key_of_row_r[:].rearrange("k h r -> k (h r)")
                for j in range(NJ):
                    n = b * NJ + j
                    wait(pe, sem("v_placed"), n + 1 - len(banks_of))
                    o, picked = banks[0:JW, banks_of[n % len(banks_of)], 0:D], rows[:, j * JS:j * JS + JW]
                    t_.matmul(o, picked, v_hi[:, b, :], start=True, stop=False)
                    t_.matmul(o, picked, v_lo[:, b, :], start=False, stop=True).then_inc(sem("v_rows_done"), 1)

            def first_layernorm(j):
                if within(j, PAIRS):
                    pe.wait_ge(sem("xn1_made"), 2 * j + 2)
                    for v in range(2):
                        for c in range(DC):
                            m = t_.transpose(banks[:, LB, c * 256 + v * P:c * 256 + (v + 1) * P],
                                             xn1[:, v, c * P:(c + 1) * P], ident[:])
                    m.then_inc(sem("xn1T_done"), 1)

            def queries(j):
                if within(j, PAIRS):
                    pe.wait_ge(sem("xn1T_hi_made"), j + 1)
                    pe.wait_ge(sem("xn1T_lo_made"), j + 1)
                    for f in range(DC):
                        for c in range(DC):
                            fs = slice(f * P, (f + 1) * P)
                            m = mm3(banks[:, QB, f * 256:(f + 1) * 256], wq_hi[:, c, fs], wq_lo[:, c, fs],
                                    xn1T_hi[:, c, :], xn1T_lo[:, c, :], c == 0, c == DC - 1)
                    m.then_inc(sem("q_done"), 1)

            pe.wait_ge(sem("ident_made"), 1)
            pe.wait_ge(sem("kT_made"), DC)
            first_layernorm(0)
            pe.wait_ge(sem("wq_split"), 1)
            queries(0)
            pe.wait_ge(sem("v_made"), NB)
            pe.wait_ge(sem("k_hi_made"), 2)
            pe.wait_ge(sem("k_lo_made"), 2)

            def step(i, u):
                t = 2 * i + u
                if isinstance(i, int) and t == 1:
                    pe.wait_ge(sem("v_placed"), 2 * NJ)
                    pe.wait_ge(sem("v_ones_made"), 2 * NB)
                if isinstance(i, int) and t == 2:
                    pe.wait_ge(sem("wo_split"), 1)
                    pe.wait_ge(sem("v_placed"), NB * NJ)
                if isinstance(i, int) and t == 3:
                    pe.wait_ge(load_wg, 16)
                if isinstance(i, int) and t == 5:
                    pe.wait_ge(sem("k_hi_made"), 2 * NB)
                    pe.wait_ge(sem("k_lo_made"), 2 * NB)

                def scores(f):
                    if within(t, NT):
                        b = batch_of(t)
                        pe.wait_ge(sem("q_hi_made"), DC * (i + 1))
                        pe.wait_ge(sem("q_lo_made"), DC * (i + 1))
                        wait(pe, sem("shifted"), 2 * (t - 1) + f + 1)
                        if f == 0 and u == 1 and within(i + 1, PAIRS):
                            pe.wait_ge(sem("xn1T_hi_made"), i + 2)
                            pe.wait_ge(sem("xn1T_lo_made"), i + 2)
                        for h in range(2):
                            ks = ds((2 * b + f) * KH + h * KC, KC)
                            m = mm3(banks[:, 2 * f + h, 0:KC], q_hi[:, f, u * P:(u + 1) * P],
                                    q_lo[:, f, u * P:(u + 1) * P], KH_hi[:, ks], KH_lo[:, ks], True, True)
                        m.then_inc(sem("scores_done"), 1)

                def transpose_probs(n):
                    if within(t - 1, NT):
                        f = n // 2
                        j0, w = 3 * (n % 2), (3, 2)[n % 2]
                        pe.wait_ge(sem("probs_made"), 2 * (t - 1) + f + 1)
                        wait(pe, sem("pT_made"), 4 * (t - 1) + n)
                        for j in range(j0, j0 + w):
                            m = t_.transpose(banks[0:JW, PT, (j - j0) * P:(j - j0 + 1) * P],
                                             probs[:, 1 - u, f * KH + j * JS:f * KH + j * JS + JW], ident[:])
                        m.then_inc(sem("pT_done"), 1)

                def weigh_values(n):
                    if within(t - 1, NT):
                        b = batch_of(t - 1)
                        f = n // 2
                        j0, w = 3 * (n % 2), (3, 2)[n % 2]
                        if n == 0:
                            wait(pe, sem("vals_made"), t - 1)
                        pe.wait_ge(sem("pT_made"), 4 * (t - 1) + n + 1)
                        for j in range(j0, j0 + w):
                            m = t_.matmul(banks[:, PV, f * VW:(f + 1) * VW], probsT[:, NJ * f + j, :],
                                          VB[:, ds(((2 * b + f) * NJ + j) * VW, VW)],
                                          start=(j == 0), stop=(j == NJ - 1))
                        if n == 3:
                            m.then_inc(sem("pv_done"), 1)

                scores(0)
                transpose_probs(0)
                if within(t - 2, NT):
                    pe.wait_ge(sem("vals_made"), t - 1)
                    wait(pe, sem("xn2T_made"), t - 3)
                    for c in range(DC):
                        m = t_.transpose(banks[:, TR, c * P:(c + 1) * P], vals[:, c * P:(c + 1) * P], ident[:])
                    m.then_inc(sem("valsT_done"), 1)
                scores(1)
                transpose_probs(1)
                weigh_values(0)
                if within(i + 1, PAIRS):
                    pe.wait_ge(sem("shifted"), 2 * t + 1)
                    if u == 0:
                        first_layernorm(i + 1)
                    else:
                        queries(i + 1)
                transpose_probs(2)
                if within(t - 2, NT):
                    pe.wait_ge(sem("valsT_hi_made"), t - 1)
                    pe.wait_ge(sem("valsT_lo_made"), t - 1)
                    wait(pe, sem("logits_made"), t - 3)
                    for c in range(DC):
                        m = mm3(banks[:, PJ, 0:D], valsT_hi[:, c, :], valsT_lo[:, c, :], wo_hi[:, c, :], wo_lo[:, c, :],
                                c == 0, c == DC - 1)
                    m.then_inc(sem("out_done"), 1)
                weigh_values(1)
                transpose_probs(3)
                if within(t - 3, NT):
                    pe.wait_ge(sem("xn2_made"), t - 2)
                    if within(t - 2, NT):
                        pe.wait_ge(sem("valsT_hi_made"), t - 1)
                        pe.wait_ge(sem("valsT_lo_made"), t - 1)
                    for c in range(DC):
                        m = t_.transpose(banks[:, TR, 256 + c * P:256 + (c + 1) * P],
                                         xn2[:, 1 - u, c * P:(c + 1) * P], ident[:])
                    m.then_inc(sem("xn2T_done"), 1)
                weigh_values(2)
                if within(t - 3, NT):
                    pe.wait_ge(sem("xn2T_made"), t - 2)
                    if within(t - 2, NT):
                        pe.wait_ge(sem("x2_made"), t - 1)
                    for c in range(DC):
                        m = t_.matmul(banks[:, PJ, 256:256 + P], xn2T[:, c, :], wg_sb[:, c, :],
                                      start=(c == 0), stop=(c == DC - 1))
                    m.then_inc(sem("logits_done"), 1)
                weigh_values(3)

            def spread_rest(b):
                if b <= 2:
                    for n in (2 * b - 2, 2 * b - 1):
                        spread(n, V_BANKS[n])

            attention_steps(pe, step, spread_rest)

            pe.wait_ge(sem("route_consts"), 9)
            pe.wait_ge(sem("sel_made"), 2 * NR)
            flat = sel[:].rearrange("p r t e -> p (r t e)")
            t_.matmul(banks[:, 0, :], ones_bf[:], sel[:].rearrange("p r t e -> p e (r t)"), start=True, stop=True).then_inc(sem("counted"), 1)
            t_.matmul(banks[:, 1, :], upper[:], flat, start=True, stop=True).then_inc(sem("counted"), 1)
            for n in range(NC):
                k, w, c = n // CH, n // CH % 2, n % CH
                if c == 0:
                    pe.wait_ge(sem("onehot_made"), 2 * (k + 1))
                    pe.wait_ge(sem("row_made"), k + 1)
                    pe.wait_ge(sem("column_made"), k + 1)
                t_.matmul(banks[:, 2, 0:2 * NS], oh_lo[:, w, c, :], oh_id[:, w, c].rearrange("p a s -> p (a s)"),
                          start=(n == 0), stop=(n == NC - 1)).then_inc(sem("placed"), 1)

            def transpose_rows(gq, c):
                if within_st(gq, c):
                    st = 10 * gq + c
                    u = c % SPE
                    pe.wait_ge(gathered[u], 32 * (2 * gq + c // SPE + 1))
                    wait(pe, sem("xT_hi_made"), st)
                    wait(pe, sem("xT_lo_made"), st)
                    for q in range(2):
                        for k in range(DC):
                            m = t_.transpose(banks[:, XT, k * 256 + q * P:k * 256 + (q + 1) * P],
                                             xg[:, u, q, k * P:(k + 1) * P], ident[:])
                    m.then_inc(sem("rows_transposed"), 1)

            def if_tokens(e, before, products):
                if before < FEW_FROM * ST_ROWS:
                    products(True)
                    return
                with pe.If(pe.value_load(tokens_e[0:1, ds(e, 1)], min_val=0, max_val=NR * N) < before + 1):
                    products(False)
                with pe.Else():
                    products(True)

            def fc1(gq, c):
                st, u, w = 10 * gq + c, c % 2, (c // SPE) % 2
                e = 2 * gq + c // SPE

                def columns(used):
                    pe.wait_ge(sem("xT_hi_made"), st + 1)
                    pe.wait_ge(sem("xT_lo_made"), st + 1)
                    pe.wait_ge(sem("w_hi_made"), 4 * e + 2)
                    pe.wait_ge(sem("w_lo_made"), 4 * e + 2)
                    for j in range(HJ):
                        if j % 2 == 0:
                            wait(pe, sem("h_made"), HJ * (st - 1) + j + 2)
                        hs, o = slice(j * P, (j + 1) * P), banks[:, j // 2, (j % 2) * 256:(j % 2 + 1) * 256]
                        if used:
                            for k in range(DC):
                                m = mm3(o, w1_hi[:, w, k, hs], w1_lo[:, w, k, hs], xT_hi[:, u, k, :],
                                        xT_lo[:, u, k, :], k == 0, k == DC - 1)
                        elif j % 2:
                            m = t_.matmul(o, w1_hi[:, w, 0, hs], xT_hi[:, u, 0, :], start=True, stop=True)
                        if j % 2:
                            m.then_inc(sem("fc1_done"), 1)

                if within_st(gq, c):
                    if_tokens(e, (c % SPE) * ST_ROWS, columns)

            def fc2(gq, c):
                st, u, w = 10 * gq + c, c % 2, (c // SPE) % 2
                e = 2 * gq + c // SPE

                def half(q, used):
                    qs, o = slice(q * P, (q + 1) * P), banks[:, YB + u, q * D:(q + 1) * D]
                    if q == 0:
                        pe.wait_ge(sem("w_hi_made"), 4 * e + 4)
                        pe.wait_ge(sem("w_lo_made"), 4 * e + 4)
                        wait(pe, sem("y_made"), st - 1)
                        if not used:
                            pe.wait_ge(sem("h_lo_made"), 4 * (st + 1))
                    if used:
                        for j in range(HJ):
                            if q == 0 and j % 2 == 0:
                                pe.wait_ge(sem("h_lo_made"), 4 * st + j // 2 + 1)
                            m = mm3(o, h_hi[:, u, j, qs], h_lo[:, u, j, qs],
                                    w2_hi[:, w, j, :], w2_lo[:, w, j, :], j == 0, j == HJ - 1)
                    else:
                        m = t_.matmul(o, h_hi[:, u, 0, qs], w2_hi[:, w, 0, :], start=True, stop=True)
                    if q == 1:
                        m.then_inc(sem("fc2_done"), 1)

                def halves(second_used):
                    if second_used:
                        half(0, True)
                    else:
                        if_tokens(e, (c % SPE) * ST_ROWS, lambda used: half(0, used))
                    half(1, second_used)

                if within_st(gq, c):
                    if_tokens(e, (c % SPE) * ST_ROWS + P, halves)

            transpose_rows(0, 0)
            pe.wait_ge(sem("tokens_counted"), 1)

            def expert_step(gq, c):
                transpose_rows(gq, c + 1)
                fc1(gq, c)
                fc2(gq, c - 1)

            expert_steps(pe, expert_step)

        @block.vector
        def _(dve):
            v = nc.vector

            def split(hi, lo, raw, name):
                v.tensor_tensor(lo[:], raw[:], hi[:].bitcast(f32), ALU.subtract).then_inc(sem(name), 1)

            def row_stats(j):
                if within(j, PAIRS):
                    for u in range(2):
                        v.bn_stats(st1[:, u, :], X[:, ds(2 * j + u, 1), :].rearrange("p a d -> p (a d)"))\
                            .then_inc(sem("st1_made"), 1)

            def aggregate(j):
                if within(j, PAIRS):
                    for u in range(2):
                        v.bn_aggr(mv1[:, u, :], st1[:, u, :]).then_inc(sem("mv1_made"), 1)
                    dve.wait_ge(sem("mv1_made"), 2 * j + 2)
                    wait(dve, sem("rstd1_made"), j)
                    v.tensor_scalar_add(var1[:], mv1[:, :, 1], EPS_LN).then_inc(sem("var1_made"), 1)

            def normalise_first(j):
                if within(j, PAIRS):
                    dve.wait_ge(sem("rstd1_made"), j + 1)
                    wait(dve, sem("xn1T_done"), j)
                    for u in range(2):
                        v.tensor_scalar(xn1[:, u, :], X[:, ds(2 * j + u, 1), :].rearrange("p a d -> p (a d)"),
                                        mv1[:, u, 0:1], rstd1[:, u:u + 1], ALU.subtract, ALU.mult)\
                            .then_inc(sem("xn1_made"), 1)

            def first_lo(j):
                if within(j, PAIRS):
                    dve.wait_ge(sem("xn1T_hi_made"), j + 1)
                    v.tensor_tensor(xn1T_lo[:].rearrange("p c t -> p (c t)"), banks[:, LB, :],
                                    xn1T_hi[:].rearrange("p c t -> p (c t)").bitcast(f32), ALU.subtract)\
                        .then_inc(sem("xn1T_lo_made"), 1)

            def queries_lo(j):
                if within(j, PAIRS):
                    for f in range(DC):
                        dve.wait_ge(sem("q_hi_made"), DC * (j + 1))
                        v.scalar_tensor_tensor(q_lo[:, f, :], banks[:, QB, f * 256:(f + 1) * 256], bq_sb[:, f:f + 1],
                                               q_hi[:, f, :].bitcast(f32), ALU.add, ALU.subtract)\
                            .then_inc(sem("q_lo_made"), 1)

            def spread_values(b):
                dve.wait_ge(sem("masks_made"), 3)
                for j in range(NJ):
                    n = b * NJ + j
                    dve.wait_ge(sem("v_rows_done"), n + 1)
                    v.tensor_tensor(VB[:].rearrange("r (b f j w) -> r b f j w", b=NB, f=2, j=NJ)[:, b, :, j, 0:P]
                                    .rearrange("r f (h d) -> r f h d", d=DH),
                                    banks[0:JW, V_BANKS[b][n % len(V_BANKS[b])], 0:D]
                                    .rearrange("r (f h d) -> r f h d", f=2, d=DH),
                                    head_of_row[:, j, :].unsqueeze(1).unsqueeze(3).to_broadcast([JW, 2, HH, DH]),
                                    ALU.mult).then_inc(sem("v_placed"), 1)

            def spread_keys(b):
                for f in range(DC):
                    v.tensor_tensor(KH_hi[:, (b * 2 + f) * KH:(b * 2 + f + 1) * KH].rearrange("p (h k) -> p h k", k=NK),
                                    kT_hi[:, f, b * NK:(b + 1) * NK].bitcast(f32).unsqueeze(1)
                                    .to_broadcast([P, HH, NK]),
                                    head_of_feature[:].unsqueeze(2).to_broadcast([P, HH, NK]),
                                    ALU.mult).then_inc(sem("k_hi_made"), 1)

            for f in range(DC):
                dve.wait_ge(sem("kT_made"), f + 1)
                v.tensor_copy(kT_hi[:, f, :], kT[:, f, :]).then_inc(sem("kT_split"), 1)
            dve.wait_ge(load_x[0], 16)
            row_stats(0)
            dve.wait_ge(sem("st1_made"), 2)
            aggregate(0)
            for f in range(DC):
                dve.wait_ge(sem("kT_split"), DC)
                v.tensor_tensor(kT_lo[:, f, :], kT[:, f, :], kT_hi[:, f, :].bitcast(f32), ALU.subtract)\
                    .then_inc(sem("kT_split"), 1)
            normalise_first(0)
            dve.wait_ge(sem("w_hi_ready"), 1)
            split(wq_hi, wq_lo, wq_sb, "wq_split")
            dve.wait_ge(load_small, 64)
            for b in range(NB):
                dve.wait_ge(sem("v_done"), 2 * (b // 2) + 2)
                v.tensor_tensor(v_sb[:, b, :], banks[0:NK, 2 + b // 2, (b % 2) * D:(b % 2 + 1) * D], bv_sb[0:NK, :],
                                ALU.add).then_inc(sem("v_made"), 1)
            first_lo(0)
            dve.wait_ge(sem("masks_made"), 3)
            spread_keys(0)
            dve.wait_ge(sem("v_hi_made"), 1)
            v.tensor_tensor(v_lo[:], v_sb[:], v_hi[:].bitcast(f32), ALU.subtract).then_inc(sem("v_lo_made"), 1)
            queries_lo(0)
            row_stats(1)
            dve.wait_ge(sem("st1_made"), 4)
            aggregate(1)
            normalise_first(1)
            dve.wait_ge(load_x[1], 16)

            def step(i, u):
                t = 2 * i + u
                if within(t - 2, NT):
                    dve.wait_ge(sem("pv_done"), t - 1)
                    pv = banks[:, PV, 0:2 * VW].rearrange("p (f w) -> p f w", w=VW)
                    v.reciprocal(rden[:], pv[:, :, P:VW]).then_inc(sem("rden_made"), 1)
                    dve.wait_ge(sem("rden_made"), t - 1)
                    v.tensor_tensor(vals[:].rearrange("p (f h d) -> p f h d", f=2, d=DH),
                                    pv[:, :, 0:P].rearrange("p f (h d) -> p f h d", d=DH),
                                    rden[:].unsqueeze(3).to_broadcast([P, 2, HH, DH]),
                                    ALU.mult).then_inc(sem("vals_made"), 1)
                def shift(f):
                    if within(t, NT):
                        s = banks[:, 2 * f:2 * f + 2, 0:KC].rearrange("p c (h k) -> p c h k", k=NK)
                        dve.wait_ge(sem("scores_done"), 2 * t + f + 1)
                        v.tensor_reduce(rowmax[:, f, :].rearrange("p (c h) -> p c h", c=2), s, AX, ALU.max)\
                            .then_inc(sem("max_made"), 1)
                    if f == 1 and u == 0:
                        row_stats(i + 2)
                    if within(t, NT):
                        dve.wait_ge(sem("max_made"), 2 * t + f + 1)
                        wait(dve, sem("pT_made"), 4 * (t - 2) + 2 * f + 2)
                        v.tensor_tensor(probs[:, u, f * KH:(f + 1) * KH].rearrange("p (c h k) -> p c h k", c=2, k=NK),
                                        s, rowmax[:, f, :].rearrange("p (c h) -> p c h", c=2).unsqueeze(3)
                                        .to_broadcast([P, 2, HH // 2, NK]),
                                        ALU.subtract).then_inc(sem("shifted"), 1)

                shift(0)
                if within(t - 2, NT):
                    dve.wait_ge(sem("valsT_hi_made"), t - 1)
                    v.tensor_tensor(valsT_lo[:].rearrange("p c q -> p (c q)"), banks[:, TR, 0:256],
                                    valsT_hi[:].rearrange("p c q -> p (c q)").bitcast(f32), ALU.subtract)\
                        .then_inc(sem("valsT_lo_made"), 1)
                shift(1)
                if u == 1:
                    queries_lo(i + 1)
                if within(t - 2, NT):
                    dve.wait_ge(sem("out_done"), t - 1)
                    dve.wait_ge(sem("x_biased"), t - 1)
                    if u == 0 and within(i + 2, PAIRS):
                        dve.wait_ge(sem("st1_made"), 2 * i + 6)
                    xt = X[:, ds(t - 2, 1), :].rearrange("p a d -> p (a d)")
                    v.tensor_tensor(xt, banks[:, PJ, 0:D], xt, ALU.add).then_inc(sem("x2_made"), 1)
                elif u == 0 and within(i + 2, PAIRS):
                    dve.wait_ge(sem("st1_made"), 2 * i + 6)
                if u == 0:
                    aggregate(i + 2)
                    first_lo(i + 1)
                if within(t - 2, NT):
                    dve.wait_ge(load_x[3], 16)
                    dve.wait_ge(sem("x2_made"), t - 1)
                    v.bn_stats(st2[:, u, :], xt).then_inc(sem("st2_made"), 1)
                    dve.wait_ge(load_x[3], 16)
                    dve.wait_ge(sem("st2_made"), t - 1)
                    v.bn_aggr(mv2[:, u, :], st2[:, u, :]).then_inc(sem("mv2_made"), 1)
                    dve.wait_ge(sem("mv2_made"), t - 1)
                    v.tensor_scalar_add(var2[:, u:u + 1], mv2[:, u, 1:2], EPS_LN).then_inc(sem("var2_made"), 1)

            def spread_rest(b):
                if b <= 2:
                    for n in (2 * b - 2, 2 * b - 1):
                        spread_values(n)
                if b == 1:
                    dve.wait_ge(sem("w_hi_ready"), 2)
                    split(wo_hi, wo_lo, wo_sb, "wo_split")
                    for n in (2, 3):
                        dve.wait_ge(load_x[n], 16)
                spread_keys(b)

            attention_steps(dve, step, spread_rest)

            done = [0]

            def then(ins):
                done[0] += 1
                ins.then_inc(sem("routed"), 1)
                dve.wait_ge(sem("routed"), done[0])

            def top_two(part, tiles):
                n = tiles.stop - tiles.start

                def over_e(x2):
                    return x2.unsqueeze(2).to_broadcast([P, n, NE])

                lg, sc, sc2, wh = (x3[:, tiles, :] for x3 in (logits, score, score2, weigh))
                dve.wait_ge(sem("logits_made"), tiles.stop)
                then(v.tensor_reduce(tsum[:, tiles], lg, AX, ALU.max))
                v.tensor_tensor(sc, lg, over_e(tsum[:, tiles]), ALU.subtract).then_inc(sem("router_shifted"), 1)
                dve.wait_ge(sem("router_exp"), part + 1)
                then(v.tensor_reduce(tsum[:, tiles], sc, AX, ALU.add))
                then(v.reciprocal(trec[:, tiles], tsum[:, tiles]))
                then(v.tensor_tensor(sc2, sc, over_e(trec[:, tiles]), ALU.mult))
                for r in range(NR):
                    then(v.tensor_reduce(tmax[:, r, tiles], sc2, AX, ALU.max))
                    then(v.tensor_tensor(wh, sc2, over_e(tmax[:, r, tiles]), ALU.is_equal))
                    then(v.tensor_tensor(wh, wh, first_of[:].unsqueeze(1).to_broadcast([P, n, NE]), ALU.mult))
                    then(v.tensor_reduce(tpick[:, r, tiles], wh, AX, ALU.max))
                    v.tensor_tensor(sel[:, r, tiles], wh, over_e(tpick[:, r, tiles]), ALU.is_equal)\
                        .then_inc(sem("sel_made"), 1)
                    if r == 0:
                        dve.wait_ge(sem("sel_made"), NR * part + 1)
                        then(v.scalar_tensor_tensor(sc2, sel[:, 0, tiles], -2.0, sc2, ALU.mult, ALU.add))

            dve.wait_ge(sem("route_consts"), 9)
            top_two(0, EARLY)
            top_two(1, LATE)
            dve.wait_ge(sem("counted"), 2)
            then(v.tensor_tensor_scan(scan_e[:].rearrange("p e c -> p (e c)"),
                                      keep_going[:].rearrange("p e c -> p (e c)"),
                                      banks[:, 0, :], 0.0, ALU.mult, ALU.add))
            v.tensor_copy(tokens_e[:], scan_e[:, :, NC - 1])\
                .then_inc(sem("tokens_counted"), 1)
            flat_place = place[:].rearrange("p r t e -> p (r t) e")
            then(v.tensor_tensor(flat_place, banks[:, 1, :].rearrange("p (c e) -> p c e", e=NE),
                                 scan_e[:].rearrange("p e c -> p c e"), ALU.add))
            then(v.tensor_tensor(flat_place, flat_place, sel[:].rearrange("p r t e -> p (r t) e"), ALU.mult))
            then(v.tensor_reduce(loc[:], flat_place, AX, ALU.add))
            then(v.tensor_scalar(kept[:], loc[:], float(CAP), None, ALU.is_le))
            pick = tpick[:].rearrange("p r t -> p (r t)")
            then(v.scalar_tensor_tensor(pos[:], pick, -float(CAP), loc[:], ALU.mult, ALU.add))
            then(v.tensor_scalar_add(pos[:], pos[:], float(NE * CAP - 1)))
            then(v.tensor_scalar(slot_lo[:], pos[:], -(P - 1) / 2.0, 1.0 / P, ALU.add, ALU.mult))
            then(v.tensor_copy(hi_i[:], slot_lo[:]))
            then(v.tensor_copy(slot_hi[:], hi_i[:]))
            then(v.scalar_tensor_tensor(slot_lo[:], slot_hi[:], -float(P), pos[:], ALU.mult, ALU.add))
            then(v.scalar_tensor_tensor(slot_hi[:], slot_hi[:], 1.0, kept[:], ALU.add, ALU.mult))
            for k in range(NC // CH):
                w, cols = k % 2, slice(k * CH, (k + 1) * CH)
                wait(dve, sem("placed"), CH * (k - 1))
                v.tensor_tensor(oh_hi[:, w], iota_hi[:].unsqueeze(1).to_broadcast([P, CH, NS]),
                                slot_hi[:, cols].unsqueeze(2).to_broadcast([P, CH, NS]), ALU.is_equal)\
                    .then_inc(sem("onehot_made"), 1)
                v.tensor_tensor(oh_lo[:, w], iota_lo[:].unsqueeze(1).to_broadcast([P, CH, P]),
                                slot_lo[:, cols].unsqueeze(2).to_broadcast([P, CH, P]), ALU.is_equal)\
                    .then_inc(sem("onehot_made"), 1)
            then(v.tensor_tensor(tsum[:], tmax[:, 0, :], tmax[:, 1, :], ALU.add))
            then(v.tensor_scalar_max(tsum[:], tsum[:], EPS_GATE))
            then(v.reciprocal(trec[:], tsum[:]))
            then(v.tensor_tensor(gates[:], tmax[:], trec[:].unsqueeze(1).to_broadcast([P, NR, NT]), ALU.mult))
            gflat = gates[:].rearrange("p r t -> p (r t)")
            v.tensor_tensor(gflat, gflat, kept[:], ALU.mult).then_inc(sem("gates_made"), 1)
            dve.wait_ge(sem("placed"), NC)
            tab = banks[:, 2, 0:2 * NS]
            pair = "p (s q) -> p s q"
            then(v.tensor_copy(empty[:], tab[:, NS:2 * NS]))
            then(v.scalar_tensor_tensor(sid[:], empty[:], float(P), tab[:, 0:NS], ALU.mult, ALU.add))
            then(v.tensor_scalar(above[:], sid[:], float(N + P), -float(N), ALU.is_ge, ALU.mult))
            then(v.tensor_tensor(sid[:], sid[:], above[:], ALU.add))
            v.tensor_scalar(slot_ids[:, :, 0, :], sid[:].rearrange(pair, q=2), -float(P), 0.0, ALU.add, ALU.max)\
                .then_inc(sem("ids_made"), 1)
            then(v.scalar_tensor_tensor(above[:], empty[:], 0.0, trash[:].rearrange("p s q -> p (s q)"),
                                        ALU.is_equal, ALU.mult))
            v.scalar_tensor_tensor(slot_ids[:, :, 1, :], sid[:].rearrange(pair, q=2), -float(P),
                                   above[:].rearrange(pair, q=2), ALU.add, ALU.add).then_inc(sem("ids_made"), 1)
            dve.wait_ge(sem("ids_made"), 2)
            then(v.scalar_tensor_tensor(sid[:], tab[:, 0:NS], float(NC), empty[:], ALU.mult, ALU.add))
            v.tensor_scalar(slot_ids[:, :, 2, :], sid[:].rearrange(pair, q=2), -1.0, 0.0, ALU.add, ALU.max)\
                .then_inc(sem("ids_made"), 1)

            def rows_lo(gq, c):
                if within_st(gq, c):
                    dve.wait_ge(sem("xT_hi_made"), 10 * gq + c + 1)
                    v.tensor_tensor(xT_lo[:, c % 2].rearrange("p c t -> p (c t)"), banks[:, XT, :],
                                    xT_hi[:, c % 2].rearrange("p c t -> p (c t)").bitcast(f32), ALU.subtract)\
                        .then_inc(sem("xT_lo_made"), 1)

            dve.wait_ge(sem("ids_made"), 3)
            rows_lo(0, 0)
            dve.wait_ge(load_b2, 16)

            def expert_step(gq, c):
                if within_st(gq, c - 2):
                    st, u = 10 * gq + c - 2, c % 2
                    e = 2 * gq + (c - 2) // SPE
                    dve.wait_ge(sem("fc2_done"), st + 1)
                    wait(dve, scattered[u], 32 * (5 * gq + (c - 2) // 2))
                    v.tensor_tensor(y_sb[:, u], banks[:, YB + u, :].rearrange("p (q d) -> p q d", d=D),
                                    b2_sb[:, ds(e, 1), :].to_broadcast([P, 2, D]), ALU.add).then_inc(sem("y_made"), 1)
                rows_lo(gq, c + 1)
                if within_st(gq, c):
                    st, u = 10 * gq + c, c % 2
                    for n in range(HJ // 2):
                        raw = hraw[:, n]
                        hi, lo = h_hi[:, u, 2 * n:2 * n + 2, :], h_lo[:, u, 2 * n:2 * n + 2, :]
                        dve.wait_ge(sem("h_made"), HJ * st + 2 * n + 2)
                        if n == 0:
                            wait(dve, sem("fc2_done"), st - 1)
                        v.tensor_copy(hi, raw).then_inc(sem("h_hi_made"), 1)
                        dve.wait_ge(sem("h_hi_made"), 4 * st + n + 1)
                        v.tensor_tensor(lo, raw, hi.bitcast(f32), ALU.subtract).then_inc(sem("h_lo_made"), 1)
                e, n = 2 * gq + c // SPE + 1, c % SPE - 1
                if n >= 0 and within(e, NE):
                    par = (c // SPE + 1) % 2
                    wait(dve, sem("fc2_done"), SPE * (e - 1))
                    dve.wait_ge(sem("w_hi_made"), 4 * e + n + 1)
                    if n == 0:
                        v.tensor_copy(b1_now[:, par, :], b1_sb[:, ds(e * HJ, HJ)]).then_inc(sem("b1_copied"), 1)
                    hi, lo, raw = w_parts(par, n)
                    v.tensor_tensor(lo, raw, hi.bitcast(f32), ALU.subtract).then_inc(sem("w_lo_made"), 1)

            dve.wait_ge(load_b1, 16)
            expert_steps(dve, expert_step)

            dve.wait_ge(sem("beta_added"), NT)

            def combine(j, c):
                s = RING * j + c
                if within(s, NG):
                    dve.wait_ge(load_res[c], 16 * (j + 1))
                    for q in range(GT):
                        v.bn_stats(st_d[:, c, q, :], res[:, ds(s * GT + q, 1), :].rearrange("p a d -> p (a d)"))\
                            .then_inc(sem("st3_made"), 1)
                if within(s - 1, NG):
                    r = (c - 1) % RING
                    dve.wait_ge(sem("rstd3_made"), s)
                    v.scalar_tensor_tensor(nmr_d[:, r, :], mv_d[:, r, :, 0], -1.0, rstd_d[:, r, :],
                                           ALU.mult, ALU.mult).then_inc(sem("nmr_made"), 1)
                if within(s, NG):
                    dve.wait_ge(sem("st3_made"), GT * (s + 1))
                if within(s - 4, NG):
                    t = ds((s - 4) * GT, GT)
                    dve.wait_ge(sem("z_scaled"), GT * (s - 3))
                    v.tensor_tensor(z[:, t, :], z[:, t, :], X[:, t, :], ALU.add).then_inc(sem("out_made"), 1)
                if within(s, NG):
                    for q in range(GT):
                        v.bn_aggr(mv_d[:, c, q, :], st_d[:, c, q, :]).then_inc(sem("mv3_made"), 1)
                    dve.wait_ge(sem("mv3_made"), GT * (s + 1))
                    v.tensor_scalar_add(var_d[:, c, :], mv_d[:, c, :, 1], EPS_LN).then_inc(sem("var3_made"), 1)

            combine_steps(dve, combine)


_OUT_SHAPE = (4, 1024, 256)


def kernel(**inputs):
    import numpy as np
    import concourse.bacc as bacc
    from concourse import mybir as mb
    from concourse.bass_utils import run_bass_kernel_spmd

    def arr(name):
        return np.asarray(inputs[name])

    x, ctx = arr("x"), arr("ctx_1024")
    heads, dh = 16, 16
    w_kv = arr("L0_xattn_w_kv").reshape(heads, 2, dh, -1)
    b_kv = arr("L0_xattn_b_kv").reshape(heads, 2, dh)
    e, h, d = arr("L0_ffn_fc1_w").shape
    data = {
        "x": x.reshape(-1, x.shape[-1]),
        "ctxT": ctx.transpose(2, 0, 1),
        "wqT": arr("L0_xattn_w_q").T,
        "bq": arr("L0_xattn_b_q").reshape(-1, 128).T,
        "wkT": w_kv[:, 0].reshape(heads * dh, -1).T,
        "bk": b_kv[:, 0].reshape(-1, 128).T,
        "wvT": w_kv[:, 1].reshape(heads * dh, -1).T,
        "bv": b_kv[:, 1].reshape(-1),
        "woT": arr("L0_xattn_w_out").T,
        "bo": arr("L0_xattn_b_out"),
        "wg": arr("L0_ffn_wg"),
        "w1T": arr("L0_ffn_fc1_w").transpose(0, 2, 1),
        "b1T": arr("L0_ffn_fc1_b").reshape(e * h // 128, 128).T,
        "w2": arr("L0_ffn_fc2_w"),
        "b2": arr("L0_ffn_fc2_b"),
        "gamma": arr("L0_ffn_ln_gamma"),
        "beta": arr("L0_ffn_ln_beta"),
    }
    nc = bacc.Bacc("TRN2", target_bir_lowering=False, num_devices=1)
    arrays, args = {}, []
    for name, a in data.items():
        a = np.ascontiguousarray(a)
        arrays[f"in_{name}"] = a
        args.append(nc.dram_tensor(f"in_{name}", a.shape, mb.dt.from_np(a.dtype), kind="ExternalInput").ap())
    out = nc.dram_tensor("out", [x.shape[0] * x.shape[1], x.shape[2]], mb.dt.float32, kind="ExternalOutput").ap()
    xattn_moe_kernel(nc, *args, out)
    r = run_bass_kernel_spmd(nc, [arrays], core_ids=[0])
    return r.results[0]["out"].reshape(_OUT_SHAPE)
```
